# Optimizing a Trainium2 kernel written in Bass

```python
import numpy as np
import jax
import jax.numpy as jnp

def _softmax(x, axis=-1):
    return jax.nn.softmax(x, axis=axis)

def _gelu(x):
    return jax.nn.gelu(x, approximate=True)

def _silu(x):
    return jax.nn.silu(x)

def _sigmoid(x):
    return jax.nn.sigmoid(x)

def _layernorm(x, axis=-1, eps=1e-05):
    m = jnp.mean(x, axis=axis, keepdims=True)
    v = jnp.var(x, axis=axis, keepdims=True)
    return (x - m) / jnp.sqrt(v + eps)

def _scatter_add(tgt, idx, src, axis=0):
    return tgt.at[idx].add(src)

def _segment_sum(src, seg, n):
    return jax.ops.segment_sum(src, seg, n)
kernel_name = 'mk_macaron_d2_jaxref_r8_234750'

def setup_inputs(seed: int=0):
    np.random.seed(seed)
    _w = jnp.asarray

    def _L0_attn_setup():
        import jax, jax.numpy as jnp
        import numpy as np
        B, S, D = (4, 256, 128)
        SCALE = 1.0 / np.sqrt(D)
        key = jax.random.key(seed)
        k1, k2, k3 = jax.random.split(key, 3)
        x = jax.random.normal(k1, (B, S, D), dtype=jnp.float32)
        bound = 1.0 / np.sqrt(D)
        W_qk = jax.random.uniform(k2, (D, D), minval=-bound, maxval=bound, dtype=jnp.float32)
        W_v = jax.random.uniform(k3, (D, D), minval=-bound, maxval=bound, dtype=jnp.float32)
        alibi_slope = jnp.full((1,), 0.5, dtype=jnp.float32)
        return {'x': x, 'W_qk': W_qk, 'W_v': W_v, 'alibi_slope': alibi_slope}
    _L0_attn_in = _L0_attn_setup()

    def _L0_ffn_setup():
        import jax, jax.numpy as jnp
        import numpy as np
        DIM = 128
        DEPTH = 2
        HEADS = 8
        DIM_HEAD = 64
        WINDOW = 64
        INNER = HEADS * DIM_HEAD
        HID = int(DIM * 4 * 2 / 3)
        B, N = (2, 1024)
        QK_SCALE = 8.0

        def shift_token(t):
            t1, t2 = jnp.split(t, 2, axis=-1)
            t2 = jnp.pad(t2, ((0, 0), (1, 0), (0, 0)))[:, :-1]
            return jnp.concatenate([t1, t2], axis=-1)

        def l2norm(t):
            return t / jnp.clip(jnp.linalg.norm(t, axis=-1, keepdims=True), 1e-12)

        def rotate_half(x):
            x1, x2 = jnp.split(x, 2, axis=-1)
            return jnp.concatenate([-x2, x1], axis=-1)

        def rotary_xpos(q, k):
            n = q.shape[-2]
            half_idx = jnp.arange(0, DIM_HEAD, 2, dtype=jnp.float32)
            inv_freq = 1.0 / 10000.0 ** (half_idx / DIM_HEAD)
            t = jnp.arange(n, dtype=jnp.float32)
            freqs = t[:, None] * inv_freq[None, :]
            freqs = jnp.concatenate([freqs, freqs], axis=-1)
            base = (half_idx + 0.4 * DIM_HEAD) / (1.4 * DIM_HEAD)
            power = (t - n // 2) / float(WINDOW // 2)
            scale = base[None, :] ** power[:, None]
            scale = jnp.concatenate([scale, scale], axis=-1)
            cos, sin = (jnp.cos(freqs), jnp.sin(freqs))
            q = q * cos * scale + rotate_half(q) * sin * scale
            k = k * cos / scale + rotate_half(k) * sin / scale
            return (q, k)

        def local_attention(q, k, v):
            b, h, n, d = q.shape
            w = n // WINDOW
            bq = q.reshape(b, h, w, WINDOW, d) * QK_SCALE
            bk = k.reshape(b, h, w, WINDOW, d)
            bv = v.reshape(b, h, w, WINDOW, d)

            def look_around(t):
                p = jnp.pad(t, ((0, 0), (0, 0), (1, 0), (0, 0), (0, 0)))
                return jnp.concatenate([p[:, :, :w], p[:, :, 1:]], axis=3)
            bk, bv = (look_around(bk), look_around(bv))
            bt = jnp.arange(n).reshape(w, WINDOW)
            btp = jnp.pad(bt, ((1, 0), (0, 0)), constant_values=-1)
            btk = jnp.concatenate([btp[:w], btp[1:]], axis=1)
            sim = jnp.einsum('bhwid,bhwjd->bhwij', bq, bk)
            i = bt[:, :, None]
            j = btk[:, None, :]
            mask = (i < j) | (i > j + WINDOW) | (j == -1)
            sim = jnp.where(mask, -jnp.finfo(sim.dtype).max, sim)
            attn = jax.nn.softmax(sim, axis=-1)
            out = jnp.einsum('bhwij,bhwjd->bhwid', attn, bv)
            return out.reshape(b, h, n, d)

        def _layer(x, wqkv, qs, ksc, wo, lg, lb, w1, b1, w2, b2):
            b, n, _ = x.shape
            h = shift_token(x)
            qkv = h @ wqkv
            q, k, v = jnp.split(qkv, 3, axis=-1)
            to_heads = lambda t: t.reshape(b, n, HEADS, DIM_HEAD).transpose(0, 2, 1, 3)
            q, k, v = (to_heads(q), to_heads(k), to_heads(v))
            q = l2norm(q) * qs
            k = l2norm(k) * ksc
            q, k = rotary_xpos(q, k)
            o = local_attention(q, k, v)
            o = o.transpose(0, 2, 1, 3).reshape(b, n, INNER)
            x = x + o @ wo
            h = shift_token(x)
            mu = h.mean(-1, keepdims=True)
            var = h.var(-1, keepdims=True)
            h = (h - mu) / jnp.sqrt(var + 1e-05) * lg + lb
            h = h @ w1 + b1
            a, g = jnp.split(h, 2, axis=-1)
            h = a * jax.nn.gelu(g, approximate=False)
            x = x + h @ w2 + b2
            return x
        key = jax.random.key(seed)
        ks = jax.random.split(key, 6)
        return {'x': jax.random.normal(ks[0], (B, N, DIM), jnp.float32), 'wqkv': jax.random.normal(ks[1], (DEPTH, DIM, 3 * INNER), jnp.float32) * 0.02, 'q_scale': jnp.ones((DEPTH, DIM_HEAD), jnp.float32), 'k_scale': jnp.ones((DEPTH, DIM_HEAD), jnp.float32), 'wo': jax.random.normal(ks[2], (DEPTH, INNER, DIM), jnp.float32) * 0.02, 'ln_g': jnp.ones((DEPTH, DIM), jnp.float32), 'ln_b': jnp.zeros((DEPTH, DIM), jnp.float32), 'w1': jax.random.normal(ks[3], (DEPTH, DIM, 2 * HID), jnp.float32) * 0.02, 'b1': jnp.zeros((DEPTH, 2 * HID), jnp.float32), 'w2': jax.random.normal(ks[4], (DEPTH, HID, DIM), jnp.float32) * 0.02, 'b2': jnp.zeros((DEPTH, DIM), jnp.float32)}
    _L0_ffn_in = _L0_ffn_setup()

    def _L1_attn_setup():
        import jax, jax.numpy as jnp
        import numpy as np
        from jax import lax
        D_MODEL, D_INNER, D_STATE, D_CONV, DT_RANK = (128, 256, 16, 4, 64)
        B, L = (1, 256)

        def _reference_tuple_inner(x, W_in, conv_w, conv_b, W_x, W_dt, b_dt, A_log, D, W_out):
            b, l, dm = x.shape
            di, n = (A_log.shape[0], A_log.shape[1])
            x_and_res = x @ W_in
            xc, res = (x_and_res[..., :di], x_and_res[..., di:])
            k = conv_w.shape[1]
            xp = jnp.pad(xc, ((0, 0), (k - 1, 0), (0, 0)))
            xconv = conv_b
            for j in range(k):
                xconv = xconv + xp[:, j:j + l, :] * conv_w[:, j]
            xs = jax.nn.silu(xconv)
            x_dbl = xs @ W_x
            dt_r = x_dbl[..., :DT_RANK]
            Bm = x_dbl[..., DT_RANK:DT_RANK + n]
            Cm = x_dbl[..., DT_RANK + n:]
            dt = jax.nn.softplus(dt_r @ W_dt + b_dt)
            A = -jnp.exp(A_log)
            dA = jnp.exp(jnp.einsum('bld,dn->bldn', dt, A))
            dBx = jnp.einsum('bld,bln->bldn', dt, Bm) * xs[..., None]

            def step(h, inp):
                dA_t, dBx_t, C_t = inp
                h = dA_t * h + dBx_t
                y = jnp.einsum('bdn,bn->bd', h, C_t)
                return (h, y)
            h0 = jnp.zeros((b, di, n), x.dtype)
            hT, ys = lax.scan(step, h0, (dA.transpose(1, 0, 2, 3), dBx.transpose(1, 0, 2, 3), Cm.transpose(1, 0, 2)))
            y = ys.transpose(1, 0, 2) + xs * D
            y = y * jax.nn.silu(res)
            out = y @ W_out
            return (out, hT)
        key = jax.random.key(seed)
        ks = jax.random.split(key, 10)
        s = lambda d: 1.0 / np.sqrt(d)
        return {'x': jax.random.normal(ks[0], (B, L, D_MODEL), jnp.float32), 'W_in': jax.random.normal(ks[1], (D_MODEL, 2 * D_INNER), jnp.float32) * s(D_MODEL), 'conv_w': jax.random.normal(ks[2], (D_INNER, D_CONV), jnp.float32) * s(D_CONV), 'conv_b': jax.random.normal(ks[3], (D_INNER,), jnp.float32) * 0.01, 'W_x': jax.random.normal(ks[4], (D_INNER, DT_RANK + 2 * D_STATE), jnp.float32) * s(D_INNER), 'W_dt': jax.random.normal(ks[5], (DT_RANK, D_INNER), jnp.float32) * s(DT_RANK), 'b_dt': jax.random.normal(ks[6], (D_INNER,), jnp.float32) * 0.01, 'A_log': jnp.log(jnp.tile(jnp.arange(1.0, D_STATE + 1.0, dtype=jnp.float32), (D_INNER, 1))), 'D': jnp.ones((D_INNER,), jnp.float32), 'W_out': jax.random.normal(ks[7], (D_INNER, D_MODEL), jnp.float32) * s(D_INNER)}
    _L1_attn_in = _L1_attn_setup()

    def _L1_ffn_setup():
        import jax, jax.numpy as jnp
        import numpy as np
        B, S, D, F, E = (2, 256, 128, 512, 8)
        LN_EPS = 1e-05

        def _xavier(key, shape, fan_in, fan_out):
            a = np.sqrt(6.0 / (fan_in + fan_out))
            return jax.random.uniform(key, shape, jnp.float32, -a, a)
        key = jax.random.key(seed)
        ks = jax.random.split(key, 8)
        tgt = jax.random.normal(ks[0], (B, S, D), jnp.float32)
        router_w = _xavier(ks[1], (E, D), D, E)
        router_b = jnp.zeros((E,), jnp.float32)
        w1 = _xavier(ks[2], (E, D, F), D, F)
        b1 = jnp.zeros((E, F), jnp.float32)
        w2 = _xavier(ks[3], (E, F, D), F, D)
        b2 = jnp.zeros((E, D), jnp.float32)
        gamma = jnp.ones((D,), jnp.float32)
        beta = jnp.zeros((D,), jnp.float32)
        return {'tgt': tgt, 'router_w': router_w, 'router_b': router_b, 'w1': w1, 'b1': b1, 'w2': w2, 'b2': b2, 'gamma': gamma, 'beta': beta}
    _L1_ffn_in = _L1_ffn_setup()
    _d = {'L0_attn_x': _L0_attn_in['x'], 'L0_attn_W_qk': _L0_attn_in['W_qk'], 'L0_attn_W_v': _L0_attn_in['W_v'], 'L0_attn_alibi_slope': _L0_attn_in['alibi_slope'], 'L0_ffn_wqkv': _L0_ffn_in['wqkv'], 'L0_ffn_q_scale': _L0_ffn_in['q_scale'], 'L0_ffn_k_scale': _L0_ffn_in['k_scale'], 'L0_ffn_wo': _L0_ffn_in['wo'], 'L0_ffn_ln_g': _L0_ffn_in['ln_g'], 'L0_ffn_ln_b': _L0_ffn_in['ln_b'], 'L0_ffn_w1': _L0_ffn_in['w1'], 'L0_ffn_b1': _L0_ffn_in['b1'], 'L0_ffn_w2': _L0_ffn_in['w2'], 'L0_ffn_b2': _L0_ffn_in['b2'], 'L1_attn_W_in': _L1_attn_in['W_in'], 'L1_attn_conv_w': _L1_attn_in['conv_w'], 'L1_attn_conv_b': _L1_attn_in['conv_b'], 'L1_attn_W_x': _L1_attn_in['W_x'], 'L1_attn_W_dt': _L1_attn_in['W_dt'], 'L1_attn_b_dt': _L1_attn_in['b_dt'], 'L1_attn_A_log': _L1_attn_in['A_log'], 'L1_attn_D': _L1_attn_in['D'], 'L1_attn_W_out': _L1_attn_in['W_out'], 'L1_ffn_router_w': _L1_ffn_in['router_w'], 'L1_ffn_router_b': _L1_ffn_in['router_b'], 'L1_ffn_w1': _L1_ffn_in['w1'], 'L1_ffn_b1': _L1_ffn_in['b1'], 'L1_ffn_w2': _L1_ffn_in['w2'], 'L1_ffn_b2': _L1_ffn_in['b2'], 'L1_ffn_gamma': _L1_ffn_in['gamma'], 'L1_ffn_beta': _L1_ffn_in['beta']}
    _x0 = _d['L0_attn_x']
    _d['L0_attn_x'] = jax.random.normal(jax.random.fold_in(jax.random.key(seed), 1), (8, 512, 128), dtype=_x0.dtype)
    del _x0
    return _d

def reference(L0_attn_x, L0_attn_W_qk, L0_attn_W_v, L0_attn_alibi_slope, L0_ffn_wqkv, L0_ffn_q_scale, L0_ffn_k_scale, L0_ffn_wo, L0_ffn_ln_g, L0_ffn_ln_b, L0_ffn_w1, L0_ffn_b1, L0_ffn_w2, L0_ffn_b2, L1_attn_W_in, L1_attn_conv_w, L1_attn_conv_b, L1_attn_W_x, L1_attn_W_dt, L1_attn_b_dt, L1_attn_A_log, L1_attn_D, L1_attn_W_out, L1_ffn_router_w, L1_ffn_router_b, L1_ffn_w1, L1_ffn_b1, L1_ffn_w2, L1_ffn_b2, L1_ffn_gamma, L1_ffn_beta):

    def _L0_attn_ref(x, W_qk, W_v, alibi_slope):
        import jax, jax.numpy as jnp
        import numpy as np
        B, S, D = (4, 256, 128)
        SCALE = 1.0 / np.sqrt(D)
        seq_len = x.shape[1]
        scores = jnp.einsum('bqe,bke->bqk', x @ W_qk, x) * SCALE
        kpos = jnp.arange(seq_len, dtype=x.dtype)[None, :]
        qpos = jnp.arange(seq_len, dtype=x.dtype)[:, None]
        scores = scores + (kpos - qpos) * alibi_slope[0]
        causal = qpos >= kpos
        scores = jnp.where(causal, scores, -jnp.inf)
        attn = jax.nn.softmax(scores, axis=-1)
        v = x @ W_v.T
        return jnp.einsum('bqk,bkd->bqd', attn, v)

    def _L0_ffn_ref(x, wqkv, q_scale, k_scale, wo, ln_g, ln_b, w1, b1, w2, b2):
        import jax, jax.numpy as jnp
        import numpy as np
        DIM = 128
        DEPTH = 2
        HEADS = 8
        DIM_HEAD = 64
        WINDOW = 64
        INNER = HEADS * DIM_HEAD
        HID = int(DIM * 4 * 2 / 3)
        B, N = (2, 1024)
        QK_SCALE = 8.0

        def shift_token(t):
            t1, t2 = jnp.split(t, 2, axis=-1)
            t2 = jnp.pad(t2, ((0, 0), (1, 0), (0, 0)))[:, :-1]
            return jnp.concatenate([t1, t2], axis=-1)

        def l2norm(t):
            return t / jnp.clip(jnp.linalg.norm(t, axis=-1, keepdims=True), 1e-12)

        def rotate_half(x):
            x1, x2 = jnp.split(x, 2, axis=-1)
            return jnp.concatenate([-x2, x1], axis=-1)

        def rotary_xpos(q, k):
            n = q.shape[-2]
            half_idx = jnp.arange(0, DIM_HEAD, 2, dtype=jnp.float32)
            inv_freq = 1.0 / 10000.0 ** (half_idx / DIM_HEAD)
            t = jnp.arange(n, dtype=jnp.float32)
            freqs = t[:, None] * inv_freq[None, :]
            freqs = jnp.concatenate([freqs, freqs], axis=-1)
            base = (half_idx + 0.4 * DIM_HEAD) / (1.4 * DIM_HEAD)
            power = (t - n // 2) / float(WINDOW // 2)
            scale = base[None, :] ** power[:, None]
            scale = jnp.concatenate([scale, scale], axis=-1)
            cos, sin = (jnp.cos(freqs), jnp.sin(freqs))
            q = q * cos * scale + rotate_half(q) * sin * scale
            k = k * cos / scale + rotate_half(k) * sin / scale
            return (q, k)

        def local_attention(q, k, v):
            b, h, n, d = q.shape
            w = n // WINDOW
            bq = q.reshape(b, h, w, WINDOW, d) * QK_SCALE
            bk = k.reshape(b, h, w, WINDOW, d)
            bv = v.reshape(b, h, w, WINDOW, d)

            def look_around(t):
                p = jnp.pad(t, ((0, 0), (0, 0), (1, 0), (0, 0), (0, 0)))
                return jnp.concatenate([p[:, :, :w], p[:, :, 1:]], axis=3)
            bk, bv = (look_around(bk), look_around(bv))
            bt = jnp.arange(n).reshape(w, WINDOW)
            btp = jnp.pad(bt, ((1, 0), (0, 0)), constant_values=-1)
            btk = jnp.concatenate([btp[:w], btp[1:]], axis=1)
            sim = jnp.einsum('bhwid,bhwjd->bhwij', bq, bk)
            i = bt[:, :, None]
            j = btk[:, None, :]
            mask = (i < j) | (i > j + WINDOW) | (j == -1)
            sim = jnp.where(mask, -jnp.finfo(sim.dtype).max, sim)
            attn = jax.nn.softmax(sim, axis=-1)
            out = jnp.einsum('bhwij,bhwjd->bhwid', attn, bv)
            return out.reshape(b, h, n, d)

        def _layer(x, wqkv, qs, ksc, wo, lg, lb, w1, b1, w2, b2):
            b, n, _ = x.shape
            h = shift_token(x)
            qkv = h @ wqkv
            q, k, v = jnp.split(qkv, 3, axis=-1)
            to_heads = lambda t: t.reshape(b, n, HEADS, DIM_HEAD).transpose(0, 2, 1, 3)
            q, k, v = (to_heads(q), to_heads(k), to_heads(v))
            q = l2norm(q) * qs
            k = l2norm(k) * ksc
            q, k = rotary_xpos(q, k)
            o = local_attention(q, k, v)
            o = o.transpose(0, 2, 1, 3).reshape(b, n, INNER)
            x = x + o @ wo
            h = shift_token(x)
            mu = h.mean(-1, keepdims=True)
            var = h.var(-1, keepdims=True)
            h = (h - mu) / jnp.sqrt(var + 1e-05) * lg + lb
            h = h @ w1 + b1
            a, g = jnp.split(h, 2, axis=-1)
            h = a * jax.nn.gelu(g, approximate=False)
            x = x + h @ w2 + b2
            return x
        for l in range(DEPTH):
            x = _layer(x, wqkv[l], q_scale[l], k_scale[l], wo[l], ln_g[l], ln_b[l], w1[l], b1[l], w2[l], b2[l])
        return x

    def _L1_attn_ref(x, W_in, conv_w, conv_b, W_x, W_dt, b_dt, A_log, D, W_out):
        import jax, jax.numpy as jnp
        import numpy as np
        from jax import lax
        D_MODEL, D_INNER, D_STATE, D_CONV, DT_RANK = (128, 256, 16, 4, 64)
        B, L = (1, 256)

        def _reference_tuple_inner(x, W_in, conv_w, conv_b, W_x, W_dt, b_dt, A_log, D, W_out):
            b, l, dm = x.shape
            di, n = (A_log.shape[0], A_log.shape[1])
            x_and_res = x @ W_in
            xc, res = (x_and_res[..., :di], x_and_res[..., di:])
            k = conv_w.shape[1]
            xp = jnp.pad(xc, ((0, 0), (k - 1, 0), (0, 0)))
            xconv = conv_b
            for j in range(k):
                xconv = xconv + xp[:, j:j + l, :] * conv_w[:, j]
            xs = jax.nn.silu(xconv)
            x_dbl = xs @ W_x
            dt_r = x_dbl[..., :DT_RANK]
            Bm = x_dbl[..., DT_RANK:DT_RANK + n]
            Cm = x_dbl[..., DT_RANK + n:]
            dt = jax.nn.softplus(dt_r @ W_dt + b_dt)
            A = -jnp.exp(A_log)
            dA = jnp.exp(jnp.einsum('bld,dn->bldn', dt, A))
            dBx = jnp.einsum('bld,bln->bldn', dt, Bm) * xs[..., None]

            def step(h, inp):
                dA_t, dBx_t, C_t = inp
                h = dA_t * h + dBx_t
                y = jnp.einsum('bdn,bn->bd', h, C_t)
                return (h, y)
            h0 = jnp.zeros((b, di, n), x.dtype)
            hT, ys = lax.scan(step, h0, (dA.transpose(1, 0, 2, 3), dBx.transpose(1, 0, 2, 3), Cm.transpose(1, 0, 2)))
            y = ys.transpose(1, 0, 2) + xs * D
            y = y * jax.nn.silu(res)
            out = y @ W_out
            return (out, hT)
        return _reference_tuple_inner(x, W_in, conv_w, conv_b, W_x, W_dt, b_dt, A_log, D, W_out)[0]

    def _L1_ffn_ref(tgt, router_w, router_b, w1, b1, w2, b2, gamma, beta):
        import jax, jax.numpy as jnp
        import numpy as np
        B, S, D, F, E = (2, 256, 128, 512, 8)
        LN_EPS = 1e-05

        def _xavier(key, shape, fan_in, fan_out):
            a = np.sqrt(6.0 / (fan_in + fan_out))
            return jax.random.uniform(key, shape, jnp.float32, -a, a)
        logits = jnp.einsum('bsd,ed->bse', tgt, router_w) + router_b
        rw = jax.nn.softmax(logits, axis=-1)
        rw = jnp.zeros_like(rw).at[..., 0].set(1.0)
        h = jax.nn.relu(jnp.einsum('bsd,edf->besf', tgt, w1) + b1[None, :, None, :])
        eo = jnp.einsum('besf,efd->besd', h, w2) + b2[None, :, None, :]
        tgt2 = jnp.einsum('besd,bse->bsd', eo, rw)
        x = tgt + tgt2
        mean = jnp.mean(x, axis=-1, keepdims=True)
        var = jnp.mean(jnp.square(x - mean), axis=-1, keepdims=True)
        return (x - mean) * jax.lax.rsqrt(var + LN_EPS) * gamma + beta
    x = L0_attn_x
    x = x + 0.5 * _L0_ffn_ref(_layernorm(x, axis=-1), L0_ffn_wqkv, L0_ffn_q_scale, L0_ffn_k_scale, L0_ffn_wo, L0_ffn_ln_g, L0_ffn_ln_b, L0_ffn_w1, L0_ffn_b1, L0_ffn_w2, L0_ffn_b2)
    x = x + _L0_attn_ref(_layernorm(x, axis=-1), L0_attn_W_qk, L0_attn_W_v, L0_attn_alibi_slope)
    x = x + 0.5 * _L0_ffn_ref(_layernorm(x, axis=-1), L0_ffn_wqkv, L0_ffn_q_scale, L0_ffn_k_scale, L0_ffn_wo, L0_ffn_ln_g, L0_ffn_ln_b, L0_ffn_w1, L0_ffn_b1, L0_ffn_w2, L0_ffn_b2)
    x = x + 0.5 * _L1_ffn_ref(_layernorm(x, axis=-1), L1_ffn_router_w, L1_ffn_router_b, L1_ffn_w1, L1_ffn_b1, L1_ffn_w2, L1_ffn_b2, L1_ffn_gamma, L1_ffn_beta)
    x = x + _L1_attn_ref(_layernorm(x, axis=-1), L1_attn_W_in, L1_attn_conv_w, L1_attn_conv_b, L1_attn_W_x, L1_attn_W_dt, L1_attn_b_dt, L1_attn_A_log, L1_attn_D, L1_attn_W_out)
    x = x + 0.5 * _L1_ffn_ref(_layernorm(x, axis=-1), L1_ffn_router_w, L1_ffn_router_b, L1_ffn_w1, L1_ffn_b1, L1_ffn_w2, L1_ffn_b2, L1_ffn_gamma, L1_ffn_beta)
    return x

_drawn_inputs = setup_inputs


def setup_inputs(seed=0):
    import zlib

    import numpy as np

    out = dict(_drawn_inputs(seed))
    spreads = {'L0_ffn_q_scale': (1.0, 0.6),
     'L0_ffn_k_scale': (1.0, 0.6),
     'L0_ffn_ln_g': (1.0, 0.6),
     'L0_ffn_ln_b': (0.0, 0.8),
     'L0_ffn_b1': (0.0, 0.8),
     'L0_ffn_b2': (0.0, 0.1),
     'L1_attn_D': (1.0, 0.6),
     'L1_ffn_router_b': (0.0, 0.1),
     'L1_ffn_b1': (0.0, 0.841),
     'L1_ffn_b2': (0.0, 0.696),
     'L1_ffn_gamma': (1.0, 0.6),
     'L1_ffn_beta': (0.0, 0.614)}
    factors = {'L0_ffn_wqkv': 2.966,
     'L0_ffn_wo': 2.954,
     'L0_ffn_w1': 4.961,
     'L0_ffn_w2': 4.886,
     'L1_attn_conv_b': 43.455,
     'L1_attn_b_dt': 64.0,
     'L1_attn_A_log': 6.409}
    for name, (base, spread) in spreads.items():
        noise = np.random.default_rng([zlib.crc32(name.encode()), seed]).standard_normal(out[name].shape)
        drawn = base * np.exp(spread * noise) if base else spread * noise
        out[name] = jnp.asarray(drawn.astype(out[name].dtype))
    for name, factor in factors.items():
        out[name] = (out[name] * factor).astype(out[name].dtype)
    return out
```

```python
import numpy as np
import concourse.bass as bass
from concourse import mybir
from contextlib import ExitStack

F32 = mybir.dt.float32
BF16 = mybir.dt.bfloat16
ALU = mybir.AluOpType
ACT = mybir.ActivationFunctionType
AX = mybir.AxisListType

P = 128
BATCH, SEQ, DIM = 8, 512, 128
TILES = SEQ // P
DEPTH, HEADS, HEAD = 2, 8, 64
INNER = HEADS * HEAD
WINDOW = 64
HID = int(DIM * 4 * 2 / 3)
HID_CHUNKS = [(c, min(P, HID - c)) for c in range(0, HID, P)]
PAIRS = INNER // P
QK_SCALE = 8.0
D_INNER, D_STATE, D_CONV, DT_RANK = 256, 16, 4, 64
CHUNKS = D_INNER // P
FF = 512
FF_CHUNKS = FF // P
LN_EPS = 1e-5
MASKED = -1e30
LANES = 2
BANK = 512


WIDTHS = {"ln": DEPTH * 2, "b1": DEPTH * 2 * 3, "e_b1": FF_CHUNKS, "conv_b": CHUNKS, "b_dt": CHUNKS, "D": CHUNKS,
          "A_log": CHUNKS * D_STATE, "conv_w": CHUNKS * D_CONV}
COLUMNS, COLUMNS_WIDTH = {}, 0
for _name, _width in WIDTHS.items():
    COLUMNS[_name] = (COLUMNS_WIDTH, _width)
    COLUMNS_WIDTH += _width


def parameter_columns(inputs):
    a = {n: np.asarray(inputs[n]) for n in inputs}
    ln = np.stack([a["L0_ffn_ln_g"], a["L0_ffn_ln_b"]], axis=1)
    b1 = a["L0_ffn_b1"].reshape(DEPTH, 2, HID)
    b1 = np.pad(b1, ((0, 0), (0, 0), (0, 3 * P - HID))).reshape(DEPTH, 2, 3, P)

    def by_chunk(v):
        return v.reshape(v.shape[0] // P, P, -1).transpose(1, 0, 2).reshape(P, -1)

    parts = {"ln": ln.transpose(2, 0, 1).reshape(P, -1), "b1": b1.transpose(3, 0, 1, 2).reshape(P, -1),
             "e_b1": by_chunk(a["L1_ffn_b1"][0]), "conv_b": by_chunk(a["L1_attn_conv_b"]),
             "b_dt": by_chunk(a["L1_attn_b_dt"]), "D": by_chunk(a["L1_attn_D"]),
             "A_log": by_chunk(a["L1_attn_A_log"]), "conv_w": by_chunk(a["L1_attn_conv_w"])}
    return np.ascontiguousarray(np.concatenate([parts[n] for n in WIDTHS], axis=1))


def constant_tables():
    f = np.float32
    half = np.arange(0, HEAD, 2, dtype=f)
    inv_freq = f(1.0) / (f(10000.0) ** (half / f(HEAD)))
    t = np.arange(SEQ, dtype=f)
    freqs = t[:, None] * inv_freq[None, :]
    freqs = np.concatenate([freqs, freqs], axis=-1)
    base = (half + f(0.4 * HEAD)) / f(1.4 * HEAD)
    power = (t - SEQ // 2) / f(WINDOW // 2)
    scale = base[None, :] ** power[:, None]
    scale = np.concatenate([scale, scale], axis=-1).astype(f)
    cos, sin = np.cos(freqs).astype(f), np.sin(freqs).astype(f)
    sign = np.concatenate([-np.ones(HEAD // 2, f), np.ones(HEAD // 2, f)])
    rotary = np.stack([cos * scale, cos / scale, sin * scale * sign, sin / scale * sign])
    rotary = rotary.reshape(2, 2, TILES, P, HEAD).transpose(3, 0, 2, 1, 4)

    row, col = np.arange(P)[:, None], np.arange(P)[None, :]
    even = row < WINDOW
    key = np.where(even & (col >= WINDOW), col - P, col)
    seen = (key <= row) & (row <= key + WINDOW)
    first = seen & (key >= 0)
    local = np.stack([np.where(m, 0.0, MASKED) for m in (first, seen)])
    local = np.tile(local[:, :, None, :], (1, 1, 4, 1)).transpose(1, 0, 2, 3)

    rel = (np.arange(SEQ)[None, :] - (SEQ - P) - row).astype(f)
    causal = np.where(rel <= 0, 0.0, MASKED).astype(f)

    spread = np.zeros((96, 2 * D_STATE, P), f)
    for part in range(3):
        for n in range(2 * D_STATE):
            spread[32 * part + n, n, :] = 1.0
    bf = mybir.dt.np(BF16)
    return {
        "c_rotary": np.ascontiguousarray(rotary, f),
        "c_local": np.ascontiguousarray(local.astype(bf)),
        "c_rel": rel,
        "c_causal": causal,
        "c_spread": np.ascontiguousarray(spread.astype(bf)),
        "c_ident": np.eye(P, dtype=f),
        "c_ident16": np.eye(P, dtype=f).astype(bf),
    }


class Engine:

    def __init__(self, name, sem):
        self.name, self.sem, self.count, self.items, self.seen = name, sem, 0, [], {}

    def wait(self, after):
        for mark in after:
            sem, value = mark
            if self.seen.get(id(sem), 0) < value:
                self.seen[id(sem)] = value
                self.items.append(("wait", sem, value))

    def do(self, method, after, *args, **kw):
        self.wait(after)
        self.count += 1
        self.items.append(("do", method, args, kw, self.sem, 1))
        return (self.sem, self.count)

    def quiet(self, method, after, *args, **kw):
        self.wait(after)
        self.items.append(("do", method, args, kw, None, 0))

    def dma(self, counter, after, out, in_):
        self.wait(after)
        self.items.append(("do", self.dma_method, (out, in_), {}, counter.sem, 16))
        return counter.next()

    def play(self, eng):
        for item in self.items:
            if item[0] == "wait":
                eng.wait_ge(item[1], item[2])
            else:
                _, method, args, kw, sem, inc = item
                ins = method(*args, **kw)
                if sem is not None:
                    ins.then_inc(sem, inc)


class DmaCount:

    def __init__(self, sem):
        self.sem, self.value = sem, 0

    def next(self):
        self.value += 16
        return (self.sem, self.value)


def weave(*gens):
    gens = list(gens)
    while gens:
        for g in list(gens):
            try:
                next(g)
                yield
            except StopIteration:
                gens.remove(g)


def macaron_kernel(nc, d, out_d):
    ctx = ExitStack()
    with ctx:
        def sb(name, shape, dt=F32):
            return ctx.enter_context(nc.sbuf_tensor(name, shape, dt))

        def sem(name):
            return ctx.enter_context(nc.semaphore(name))

        pe = Engine("pe", sem("pe_done"))
        dve = Engine("dve", sem("dve_done"))
        act = Engine("act", sem("act_done"))
        pool = Engine("pool", sem("pool_done"))
        sp = Engine("sp", sem("sp_done"))
        sp.dma_method = nc.sync.dma_start
        V, A, G, T = nc.vector, nc.scalar, nc.gpsimd, nc.tensor

        ident = sb("ident", [P, P])
        ident16 = sb("ident16", [P, P], BF16)
        local_mask = sb("local_mask", [P, 2, 4 * P], BF16)
        rel = sb("rel", [P, SEQ])
        alibi = sb("alibi", [P, SEQ])
        slope = sb("slope", [P, 1])
        spread = sb("spread", [96, 2 * D_STATE, P], BF16)
        rot_base = sb("rot_base", [P, 2, TILES, 2, HEAD])
        rot = [sb(f"rot{l}", [P, 2, TILES, 2, HEAD]) for l in range(DEPTH)]
        qk_gain = sb("qk_gain", [P, DEPTH, 2, HEAD])
        wqkv = sb("wqkv", [P, DEPTH, 3 * INNER])
        wo = sb("wo", [P, DEPTH, PAIRS, DIM])
        columns = sb("columns", [P, COLUMNS_WIDTH])
        col = {n: columns[:, at:at + w] for n, (at, w) in COLUMNS.items()}
        lnT = col["ln"].rearrange("p (l a) -> p l a", l=DEPTH)
        w1 = sb("w1", [P, DEPTH, 2 * HID])
        b1T = col["b1"].rearrange("p (l a c) -> p l a c", l=DEPTH, a=2)
        w2 = sb("w2", [P, DEPTH, 3, DIM])
        Wqk = sb("Wqk", [P, DIM])
        WvT = sb("WvT", [P, DIM])
        W_in = sb("W_in", [P, 2 * D_INNER])
        conv_w = col["conv_w"].rearrange("p (c j) -> p c j", c=CHUNKS)
        conv_b = col["conv_b"]
        W_x = sb("W_x", [P, CHUNKS, DT_RANK + 2 * D_STATE])
        W_dt = sb("W_dt", [DT_RANK, D_INNER])
        b_dt = col["b_dt"]
        negA = sb("negA", [P, CHUNKS, D_STATE])
        skipD = col["D"]
        W_out = sb("W_out", [P, CHUNKS, DIM])
        e_w1 = sb("e_w1", [P, FF])
        e_b1 = col["e_b1"]
        e_w2 = sb("e_w2", [P, FF_CHUNKS, DIM])
        e_b2 = sb("e_b2", [P, DIM])
        gamma = sb("gamma", [P, DIM])
        beta = sb("beta", [P, DIM])
        neg_half = sb("neg_half", [P, 16])

        loaded = DmaCount(sem("weights_loaded"))

        def load(dst, src):
            sp.dma(loaded, [], dst, src)

        class Lane:
            pass

        def new_lane(i):
            L = Lane()
            L.x = sb(f"x{i}", [P, TILES, DIM])
            L.y = sb(f"y{i}", [P, TILES, DIM])
            L.xn = sb(f"xn{i}", [P, TILES, DIM])
            L.shifted = sb(f"shifted{i}", [P, TILES, DIM])
            L.hT = sb(f"hT{i}", [P, SEQ])
            L.bc3 = sb(f"bc3{i}", [96, SEQ], BF16)
            L.stats = sb(f"stats{i}", [P, TILES, 6])
            L.mv = sb(f"mv{i}", [P, TILES, 2])
            L.rstd = sb(f"rstd{i}", [P, TILES])
            L.ss = sb(f"ss{i}", [P, 16])
            L.rn = sb(f"rn{i}", [P, 16])
            L.mx = sb(f"mx{i}", [P, HEADS])
            L.rs = sb(f"rs{i}", [P, HEADS])
            L.work = sb(f"work{i}", [P, 14400])
            L.q = ctx.enter_context(nc.psum_tensor(f"q_banks{i}", [P, 2, BANK], F32))
            L.t = ctx.enter_context(nc.psum_tensor(f"t_banks{i}", [P, 2, BANK], F32))
            L.x_in = DmaCount(sem(f"x_in{i}"))
            L.x_out = DmaCount(sem(f"x_out{i}"))
            L.shift_in = DmaCount(sem(f"shift_in{i}"))
            L.v_in = [DmaCount(sem(f"v_in{i}_{t}")) for t in range(TILES)]

            at = [0]

            def cut(*shape):
                n = int(np.prod(shape))
                ap = L.work[:, at[0]:at[0] + n]
                at[0] += n
                assert at[0] <= 14400
                if len(shape) == 2:
                    ap = ap.rearrange("p (a b) -> p a b", a=shape[0])
                elif len(shape) == 3:
                    ap = ap.rearrange("p (a b c) -> p a b c", a=shape[0], b=shape[1])
                return ap

            L.sq = L.ts = cut(16, HEAD)
            L.tq = cut(16, HEAD)
            L.tc = cut(16, HEAD)
            L.qT = [cut(PAIRS, P) for _ in range(2)]
            L.kT = cut(PAIRS, SEQ)
            L.V = cut(TILES, HEADS, HEAD + 1)
            L.Vc = cut(TILES, HEADS, HEAD + 1)
            L.prob = cut(8, P)
            L.probT = cut(8, P)
            L.o = L.prob[:, 0:4, :]
            L.oT = L.probT[:, 0:4, :]
            at[0] = 0
            L.hid = cut(3, SEQ)
            L.gelu = [cut(SEQ) for _ in range(2)]
            at[0] = 0
            L.uT = cut(SEQ)
            L.va = cut(TILES, DIM)
            L.ap = [cut(SEQ) for _ in range(2)]
            L.apT = [cut(TILES, P) for _ in range(2)]
            at[0] = 0
            L.xc = cut(CHUNKS, SEQ + D_CONV - 1)
            L.gate = cut(CHUNKS, SEQ)
            L.xs = cut(CHUNKS, SEQ)
            L.dt = cut(CHUNKS, SEQ)
            L.dtx = cut(CHUNKS, SEQ)
            L.dA = [cut(CHUNKS, SEQ) for _ in range(2)]
            L.dBx = cut(CHUNKS, SEQ)
            L.h = [cut(CHUNKS, SEQ) for _ in range(2)]
            L.hC = [cut(CHUNKS, SEQ) for _ in range(2)]
            L.Cs = [cut(SEQ) for _ in range(2)]
            L.tmp = L.dBx
            at[0] = 0
            L.eh = cut(FF_CHUNKS, SEQ)
            L.r = cut(TILES, DIM)
            return L

        lanes = [new_lane(i) for i in range(LANES)]
        x_dram = d["L0_attn_x"].rearrange("b (t p) d -> b p t d", p=P)
        out_dram = out_d.rearrange("b (t p) d -> b p t d", p=P)

        for i, L in enumerate(lanes):
            L.x_here = sp.dma(L.x_in, [], L.x[:], x_dram[i])
        load(ident[:], d["c_ident"])
        load(ident16[:], d["c_ident16"])
        load(wqkv[:], d["L0_ffn_wqkv"].rearrange("l k n -> k l n"))
        load(rot_base[:], d["c_rotary"])
        for l in range(DEPTH):
            load(qk_gain[:, l, 0, :], d["L0_ffn_q_scale"][l].partition_broadcast(P))
            load(qk_gain[:, l, 1, :], d["L0_ffn_k_scale"][l].partition_broadcast(P))
        load(local_mask[:], d["c_local"].rearrange("p a b c -> p a (b c)"))
        load(wo[:], d["L0_ffn_wo"].rearrange("l (c p) n -> p l c n", p=P))
        load(w1[:], d["L0_ffn_w1"].rearrange("l k n -> k l n"))
        for c, (c0, n) in enumerate(HID_CHUNKS):
            for l in range(DEPTH):
                load(w2[0:n, l, c, :], d["L0_ffn_w2"][l, c0:c0 + n, :])
        last_rows = HID_CHUNKS[-1][1]
        for l in range(DEPTH):
            load(w2[last_rows:last_rows + 1, l, 2, :], d["L0_ffn_b2"][l:l + 1, :])
        load(columns[:], d["columns"])
        load(Wqk[:], d["L0_attn_W_qk"])
        load(WvT[:], d["WvT"])
        load(slope[:], d["L0_attn_alibi_slope"].partition_broadcast(P))
        load(rel[:], d["c_rel"])
        load(alibi[:], d["c_causal"])
        load(e_w1[:], d["L1_ffn_w1"][0])
        load(e_w2[:], d["L1_ffn_w2"][0].rearrange("(c p) n -> p c n", p=P))
        load(e_b2[:], d["L1_ffn_b2"][0].partition_broadcast(P))
        load(gamma[:], d["L1_ffn_gamma"].partition_broadcast(P))
        load(beta[:], d["L1_ffn_beta"].partition_broadcast(P))
        load(W_in[:], d["L1_attn_W_in"])
        load(W_x[:], d["L1_attn_W_x"].rearrange("(c p) n -> p c n", p=P))
        load(W_dt[:], d["L1_attn_W_dt"])
        load(W_out[:], d["L1_attn_W_out"].rearrange("(c p) n -> p c n", p=P))
        load(spread[:], d["c_spread"])
        weights = (loaded.sem, loaded.value)

        H2 = HEAD // 2
        const = pool.do(G.memset, [], neg_half[:], -0.5)
        for l in range(DEPTH):
            g = qk_gain[:, l].unsqueeze(1)
            full = [P, TILES, 2, HEAD]
            half = [P, TILES, 2, H2]
            dve.do(V.tensor_tensor, [weights], out=rot[l][:, 0], in0=rot_base[:, 0],
                   in1=g.to_broadcast(full), op=ALU.mult)
            dve.do(V.tensor_tensor, [], out=rot[l][:, 1, :, :, 0:H2], in0=rot_base[:, 1, :, :, 0:H2],
                   in1=g[:, :, :, H2:HEAD].to_broadcast(half), op=ALU.mult)
            dve.do(V.tensor_tensor, [], out=rot[l][:, 1, :, :, H2:HEAD], in0=rot_base[:, 1, :, :, H2:HEAD],
                   in1=g[:, :, :, 0:H2].to_broadcast(half), op=ALU.mult)
        dve.do(V.scalar_tensor_tensor, [], out=alibi[:], in0=rel[:], scalar=slope[:, 0:1],
               in1=alibi[:], op0=ALU.mult, op1=ALU.add)
        A_log = col["A_log"].rearrange("p (c n) -> p c n", c=CHUNKS)
        exp_A = act.do(A.activation, [weights], negA[:], A_log, ACT.Exp)
        tables = dve.do(V.tensor_scalar, [exp_A], out=negA[:], in0=negA[:], scalar1=-1.0, scalar2=None,
                        op0=ALU.mult)
        ready = [weights, tables, const]


        def layer_norm(L, src, dst, after):
            for t in range(TILES):
                m = dve.do(V.bn_stats, after, L.stats[:, t, :], src[:, t, :])
            for t in range(TILES):
                m = dve.do(V.bn_aggr, [m], L.mv[:, t, :], L.stats[:, t, :])
            yield
            m = dve.do(V.tensor_scalar, [m], out=L.rstd[:], in0=L.mv[:, :, 1], scalar1=LN_EPS, scalar2=None,
                       op0=ALU.add)
            m = pool.do(G.tensor_tensor, [m, const], out=L.rstd[:], in0=L.rstd[:], in1=neg_half[:, 0:TILES],
                        op=ALU.pow)
            yield
            for t in range(TILES):
                m = dve.do(V.tensor_scalar, [m], out=dst[:, t, :], in0=src[:, t, :],
                           scalar1=L.mv[:, t, 0:1], scalar2=L.rstd[:, t:t + 1],
                           op0=ALU.subtract, op1=ALU.mult)
            L.normed = m
            yield

        def to_features(L, src, bank, after):
            for t in range(TILES):
                m = pe.do(T.transpose, after, bank[:, t * P:(t + 1) * P], src[:, t, :], ident[:])
            return m

        def project(L, l, t, after):
            hT = L.hT[:, t * P:(t + 1) * P]
            q0, q1 = L.q[:, 0, :], L.q[:, 1, :]
            free = L.q_free
            pe.do(T.matmul, after + free, q0, lhsT=hT, rhs=wqkv[:, l, 0:INNER], start=True, stop=True)
            qk = pe.do(T.matmul, [], q1, lhsT=hT, rhs=wqkv[:, l, INNER:2 * INNER], start=True, stop=True)
            yield
            qk_view = L.q[:, :, :].rearrange("p a (h d) -> p (a h) d", d=HEAD)
            squared = act.do(A.activation, [qk] + L.ts_read, L.sq, qk_view, ACT.Square)
            m = dve.do(V.tensor_reduce, [squared], out=L.ss[:], in_=L.sq, axis=AX.X, op=ALU.add)
            m = dve.do(V.tensor_scalar, [m], out=L.ss[:], in0=L.ss[:], scalar1=1e-24, scalar2=None, op0=ALU.max)
            norm = pool.do(G.tensor_tensor, [m, const], out=L.rn[:], in0=L.ss[:], in1=neg_half[:], op=ALU.pow)
            yield
            unit = dve.do(V.tensor_tensor, [norm, qk] + L.tq_read, out=L.tq, in0=qk_view,
                          in1=L.rn[:].unsqueeze(2).to_broadcast([P, 16, HEAD]), op=ALU.mult)
            v = pe.do(T.matmul, [unit], q0, lhsT=hT, rhs=wqkv[:, l, 2 * INNER:3 * INNER], start=True, stop=True)
            yield
            tq4 = L.tq.rearrange("p (a h) d -> p a h d", a=2)
            ts4 = L.ts.rearrange("p (a h) d -> p a h d", a=2)
            tc4 = L.tc.rearrange("p (a h) d -> p a h d", a=2)
            cos = rot[l][:, 0, t].unsqueeze(2)
            sin = rot[l][:, 1, t].unsqueeze(2)
            cosined = pool.do(G.tensor_tensor, [unit] + L.ts_read, out=tc4, in0=tq4,
                              in1=cos.to_broadcast([P, 2, HEADS, HEAD]), op=ALU.mult)
            hb = [P, 2, HEADS, H2]
            dve.do(V.tensor_tensor, [unit], out=ts4[:, :, :, 0:H2], in0=tq4[:, :, :, H2:HEAD],
                   in1=sin[:, :, :, 0:H2].to_broadcast(hb), op=ALU.mult)
            sined = dve.do(V.tensor_tensor, [], out=ts4[:, :, :, H2:HEAD], in0=tq4[:, :, :, 0:H2],
                           in1=sin[:, :, :, H2:HEAD].to_broadcast(hb), op=ALU.mult)
            L.tq_read = [cosined]
            v_copied = act.do(A.activation, [v] + L.v_free[t], L.V[:, t, :, 0:HEAD],
                              q0.rearrange("p (h d) -> p h d", d=HEAD), ACT.Copy)
            v_dma = sp.dma(L.v_in[t], [v_copied] + L.v_free[t], L.Vc[0:WINDOW, t], L.V[0:WINDOW, t])
            if t > 0:
                v_dma = sp.dma(L.v_in[t], [], L.Vc[WINDOW:P, t], L.V[WINDOW:P, t - 1])
            L.v_here[t] = [v_copied, v_dma]
            yield
            tcf = L.tc.rearrange("p (c h) d -> p c (h d)", h=2)
            tsf = L.ts.rearrange("p (c h) d -> p c (h d)", h=2)
            for side, bank, wait in ((0, q1, [cosined, sined]), (1, q0, [v_copied])):
                for c in range(PAIRS):
                    dst = bank[:, c * P:(c + 1) * P]
                    pe.quiet(T.matmul, wait, dst, lhsT=tcf[:, side * PAIRS + c, :], rhs=ident[:],
                             is_transpose=True, start=True, stop=False)
                    m = pe.do(T.matmul, [], dst, lhsT=tsf[:, side * PAIRS + c, :], rhs=ident[:],
                              is_transpose=True, start=False, stop=True)
                if side == 0:
                    q_ready = m
            L.ts_read = [m]
            yield
            qT = L.qT[t % 2]
            q_copied = act.do(A.activation, [q_ready] + L.qT_read[t % 2], qT, q1.rearrange("p (c n) -> p c n", c=PAIRS), ACT.Copy)
            k_copied = act.do(A.activation, [m], L.kT[:, :, t * P:(t + 1) * P],
                              q0.rearrange("p (c n) -> p c n", c=PAIRS), ACT.Copy)
            L.q_free = [k_copied]
            L.qk_here[t] = [q_copied, k_copied]
            yield

        def local_attention(L, l, t):
            s0, s1 = L.t[:, 0, :], L.t[:, 1, :]
            qT = L.qT[t % 2]
            mask = local_mask[:, min(t, 1), :]
            lo = t * P
            pe.quiet(T.matmul, L.t_free + L.qk_here[t], s0, lhsT=ident16[:], rhs=mask, start=True, stop=False,
                     skip_group_check=True)
            pe.quiet(T.matmul, [], s1, lhsT=ident16[:], rhs=mask, start=True, stop=False, skip_group_check=True)
            for h in range(HEADS):
                rows = slice((h % 2) * HEAD, (h % 2 + 1) * HEAD)
                bank = L.t[:, h % 2, :]
                c0 = (h // 2) * P
                k = L.kT[rows, h // 2, :]
                q = qT[rows, h // 2, :]
                before = lo - WINDOW if t > 0 else lo
                pe.quiet(T.matmul, [], bank[:, c0:c0 + WINDOW], lhsT=q, rhs=k[:, lo:lo + WINDOW],
                         start=False, stop=True, skip_group_check=True)
                pe.quiet(T.matmul, [], bank[0:WINDOW, c0 + WINDOW:c0 + P], lhsT=q[:, 0:WINDOW],
                         rhs=k[:, before:before + WINDOW], start=False, stop=True, skip_group_check=True)
                m = pe.do(T.matmul, [], bank[WINDOW:P, c0 + WINDOW:c0 + P], lhsT=q[:, WINDOW:P],
                          rhs=k[:, lo + WINDOW:lo + P], start=False, stop=True, skip_group_check=True)
                if h % 4 == 3:
                    yield
            scored = m
            L.qT_read[t % 2] = [scored]
            s = L.t[:, :, :].rearrange("p a (j n) -> p (a j) n", n=P)
            m = dve.do(V.tensor_reduce, [scored], out=L.mx[:], in_=s, axis=AX.X, op=ALU.max)
            lowered = dve.do(V.tensor_tensor, [m] + L.prob_read, out=L.prob, in0=s,
                             in1=L.mx[:].unsqueeze(2).to_broadcast([P, 8, P]), op=ALU.subtract)
            yield
            raised = act.do(A.activation, [lowered], L.prob, L.prob, ACT.Exp, scale=QK_SCALE)
            yield
            for b in range(8):
                m = pe.do(T.transpose, [raised, lowered], L.t[:, b // 4, (b % 4) * P:(b % 4 + 1) * P],
                          L.prob[:, b, :], ident[:])
            yield
            copied = act.do(A.activation, [m] + L.probT_read, L.probT,
                            L.t[:, :, :].rearrange("p a (j n) -> p (a j) n", n=P), ACT.Copy)
            yield
            W1 = HEAD + 1
            for b in range(8):
                h = 2 * (b % 4) + b // 4
                dst = L.t[:, b // 4, (b % 4) * W1:(b % 4 + 1) * W1]
                pe.quiet(T.matmul, [copied] + L.v_here[t], dst[0:WINDOW], lhsT=L.probT[:, b, 0:WINDOW],
                         rhs=L.Vc[:, t, h, :], start=True, stop=True)
                m = pe.do(T.matmul, [], dst[WINDOW:P], lhsT=L.probT[:, b, WINDOW:P],
                          rhs=L.V[:, t, h, :], start=True, stop=True)
                if b % 4 == 3:
                    yield
            L.v_free[t] = [m]
            if t + 1 < TILES:
                L.v_free[t + 1] = [m]
            o = L.t[:, :, 0:4 * W1].rearrange("p a (j w) -> p a j w", w=W1)
            rs = L.rs[:].rearrange("p (a j) -> p a j", a=2)
            m = dve.do(V.reciprocal, [m], rs, o[:, :, :, HEAD])
            divided = dve.do(V.tensor_tensor, [m],
                             out=L.o.rearrange("p j (a d) -> p a j d", a=2), in0=o[:, :, :, 0:HEAD],
                             in1=rs.unsqueeze(3).to_broadcast([P, 2, 4, HEAD]), op=ALU.mult)
            yield
            for c in range(PAIRS):
                m = pe.do(T.transpose, [divided], s0[:, c * P:(c + 1) * P], L.o[:, c, :], ident[:])
            L.prob_read = [m]
            oT_copied = act.do(A.activation, [m], L.oT, s0.rearrange("p (c n) -> p c n", c=PAIRS), ACT.Copy)
            yield
            for c in range(PAIRS):
                m = pe.do(T.matmul, [oT_copied, divided], s1[:, 0:DIM], lhsT=L.oT[:, c, :], rhs=wo[:, l, c, :],
                          start=(c == 0), stop=(c == PAIRS - 1))
            L.probT_read = [m]
            added = dve.do(V.tensor_tensor, [m], out=L.y[:, t, :], in0=s1[:, 0:DIM], in1=L.y[:, t, :], op=ALU.add)
            L.t_free = [added, oT_copied]
            L.y_ready[t] = added
            yield

        def transformer_layer(L, l):
            q0, q1, t0, t1 = L.q[:, 0, :], L.q[:, 1, :], L.t[:, 0, :], L.t[:, 1, :]
            m = to_features(L, L.y, q0, L.y_done + L.q_free)
            a = act.do(A.activation, [m], L.hT[0:HEAD, :], q0[0:HEAD, :], ACT.Copy)
            b = act.do(A.activation, [], L.hT[HEAD:P, 1:SEQ], q0[HEAD:P, 0:SEQ - 1], ACT.Copy)
            z = dve.do(V.memset, L.y_done, L.hT[HEAD:P, 0:1], 0.0)
            L.q_free = [b, z]
            L.y_ready = [None] * TILES
            L.v_here, L.qk_here = [None] * TILES, [None] * TILES
            yield
            yield from project(L, l, 0, [a, b, z])
            for t in range(TILES):
                if t + 1 < TILES:
                    yield from weave(local_attention(L, l, t), project(L, l, t + 1, [a, b, z]))
                else:
                    yield from local_attention(L, l, t)
            y_all = list(L.y_ready)
            sh = pool.do(G.tensor_copy, y_all, L.shifted[:, :, 0:HEAD], L.y[:, :, 0:HEAD])
            sp.dma(L.shift_in, y_all, L.shifted[1:113, :, HEAD:DIM], L.y[0:112, :, HEAD:DIM])
            sp.dma(L.shift_in, [], L.shifted[113:128, :, HEAD:DIM], L.y[112:127, :, HEAD:DIM])
            sd = sp.dma(L.shift_in, [], L.shifted[0:1, 1:TILES, HEAD:DIM], L.y[127:128, 0:TILES - 1, HEAD:DIM])
            yield
            yield from layer_norm(L, L.shifted, L.xn, [sh, sd])
            m = to_features(L, L.xn, q0, [L.normed] + L.q_free)
            hT = act.do(A.activation, [m], L.hT[:], q0, ACT.Identity, bias=lnT[:, l, 1:2], scale=lnT[:, l, 0:1])
            ones = dve.do(V.memset, L.y_ready, L.hid[HEAD:P, 2, :], 1.0)
            yield
            banks = [(q1, t0), (t1, q0), (q1, t0)]
            freed = {0: L.q_free + L.t_free, 1: L.t_free + [hT], 2: []}
            hid_ready = []
            for c, (c0, n) in enumerate(HID_CHUNKS):
                ba, bg = banks[c]
                g = pe.do(T.matmul, [hT] + freed[c], bg[0:n, :], lhsT=w1[:, l, HID + c0:HID + c0 + n], rhs=L.hT[:],
                          start=True, stop=True)
                u = pe.do(T.matmul, [], ba[0:n, :], lhsT=w1[:, l, c0:c0 + n], rhs=L.hT[:], start=True, stop=True)
                ge = act.do(A.activation, [g] + (hid_ready[0:1] if c == 2 else []), L.gelu[c % 2][0:n, :],
                            bg[0:n, :], ACT.Gelu, bias=b1T[0:n, l, 1, c:c + 1])
                hd = dve.do(V.scalar_tensor_tensor, [u, ge, ones], out=L.hid[0:n, c, :], in0=ba[0:n, :],
                            scalar=b1T[0:n, l, 0, c:c + 1], in1=L.gelu[c % 2][0:n, :],
                            op0=ALU.add, op1=ALU.mult)
                hid_ready.append(hd)
                if c == 0:
                    freed[2] = [ge, hd]
                yield
            for t in range(TILES):
                for c, (c0, n) in enumerate(HID_CHUNKS):
                    k = n + 1 if c == 2 else n
                    m = pe.do(T.matmul, hid_ready, t1[:, t * P:(t + 1) * P], lhsT=L.hid[0:k, c, t * P:(t + 1) * P],
                              rhs=w2[0:k, l, c, :], start=(c == 0), stop=(c == 2))
            yield
            m = dve.do(V.tensor_tensor, [m], out=L.y[:], in0=t1.rearrange("p (t n) -> p t n", t=TILES),
                       in1=L.y[:], op=ALU.add)
            L.q_free = [hd, ge, m]
            L.t_free = [m, ge, hd]
            L.ts_read = L.tq_read = L.prob_read = L.probT_read = [m]
            L.qT_read = [[m], [m]]
            L.v_free = [[m] for _ in range(TILES)]
            L.y_done = [m]
            yield

        def macaron_transformer(L):
            ones = pool.do(G.memset, L.x_done + ready, L.V[:, :, :, HEAD:HEAD + 1], 1.0)
            z1 = pool.do(G.memset, [], L.Vc[:, 0, :, :], 0.0)
            z2 = pool.do(G.memset, [], L.shifted[:, 0, HEAD:DIM], 0.0)
            start = L.x_done + [ones, z1, z2]
            yield from layer_norm(L, L.x, L.y, start)
            L.y_done = [L.normed]
            L.ts_read = L.tq_read = L.prob_read = L.probT_read = [L.normed, z1]
            L.qT_read = [[], []]
            L.v_free = [[z1, ones] for _ in range(TILES)]
            for l in range(DEPTH):
                yield from transformer_layer(L, l)
            m = dve.do(V.scalar_tensor_tensor, L.y_done, out=L.x[:], in0=L.y[:], scalar=0.5, in1=L.x[:],
                       op0=ALU.mult, op1=ALU.add)
            L.x_done = [m]
            yield

        def alibi_attention(L):
            q0, q1, t0, t1 = L.q[:, 0, :], L.q[:, 1, :], L.t[:, 0, :], L.t[:, 1, :]
            yield from layer_norm(L, L.x, L.xn, L.x_done)
            m = to_features(L, L.xn, q0, [L.normed] + L.q_free)
            xT = act.do(A.activation, [m], L.hT[:], q0, ACT.Copy)
            yield
            m = pe.do(T.matmul, [xT] + L.q_free, q1, lhsT=Wqk[:], rhs=L.hT[:], start=True, stop=True)
            uT = act.do(A.activation, [m], L.uT, q1, ACT.Copy)
            for t in range(TILES):
                m = pe.do(T.matmul, L.t_free, t0[:, t * P:(t + 1) * P], lhsT=L.hT[:, t * P:(t + 1) * P], rhs=WvT[:],
                          start=True, stop=True)
            va = act.do(A.activation, [m], L.va, t0.rearrange("p (t n) -> p t n", t=TILES), ACT.Copy)
            yield
            scale = float(np.float32(1.0 / np.sqrt(128)))
            s_free = [[xT], [va]]
            p_free = [[uT], L.t_free]
            o_read = [[], []]
            for t in range(TILES):
                i = t % 2
                S, PT = (q0, q1) if i == 0 else (t0, t1)
                n = (t + 1) * P
                m = pe.do(T.matmul, [uT, xT] + s_free[i], S[:, 0:n], lhsT=L.uT[:, t * P:(t + 1) * P],
                          rhs=L.hT[:, 0:n], start=True, stop=True)
                sc = dve.do(V.scalar_tensor_tensor, [m] + p_free[i], out=L.ap[i][:, 0:n], in0=S[:, 0:n], scalar=scale,
                            in1=alibi[:, SEQ - n:SEQ], op0=ALU.mult, op1=ALU.add)
                m = dve.do(V.tensor_reduce, [sc] + o_read[i], out=L.mx[:, i:i + 1], in_=L.ap[i][:, 0:n],
                           axis=AX.X, op=ALU.max, negate=True)
                yield
                ex = act.do(A.activation, [m], L.ap[i][:, 0:n], L.ap[i][:, 0:n], ACT.Exp,
                            bias=L.mx[:, i:i + 1], accum_out=L.rs[:, i:i + 1])
                for k in range(t + 1):
                    m = pe.do(T.transpose, [ex] + p_free[i], PT[:, k * P:(k + 1) * P],
                              L.ap[i][:, k * P:(k + 1) * P], ident[:])
                pT = act.do(A.activation, [m], L.apT[i][:, 0:t + 1, :],
                            PT[:, 0:n].rearrange("p (t n) -> p t n", t=t + 1), ACT.Copy)
                yield
                for k in range(t + 1):
                    m = pe.do(T.matmul, [pT, va, sc], S[:, 0:DIM], lhsT=L.apT[i][:, k, :], rhs=L.va[:, k, :],
                              start=(k == 0), stop=(k == t))
                r = dve.do(V.reciprocal, [ex], L.rs[:, 2 + i:3 + i], L.rs[:, i:i + 1])
                xd = dve.do(V.scalar_tensor_tensor, [m, r], out=L.x[:, t, :], in0=S[:, 0:DIM],
                            scalar=L.rs[:, 2 + i:3 + i], in1=L.x[:, t, :], op0=ALU.mult, op1=ALU.add)
                s_free[i] = [xd]
                p_free[i] = [pT, m]
                o_read[i] = [xd]
                yield
            L.x_done = [xd]
            L.q_free = L.t_free = [xd, pT]

        def expert_ffn(L):
            banks = [L.q[:, 1, :], L.t[:, 0, :], L.t[:, 1, :], L.q[:, 0, :]]
            q0, q1 = banks[3], banks[0]
            yield from layer_norm(L, L.x, L.xn, L.x_done)
            m = to_features(L, L.xn, q0, [L.normed] + L.q_free)
            xT = act.do(A.activation, [m], L.hT[:], q0, ACT.Copy)
            yield
            for c in range(FF_CHUNKS):
                m = pe.do(T.matmul, [xT] + L.q_free + L.t_free, banks[c], lhsT=e_w1[:, c * P:(c + 1) * P],
                          rhs=L.hT[:], start=True, stop=True)
                h = act.do(A.activation, [m], L.eh[:, c, :], banks[c], ACT.Relu, bias=e_b1[:, c:c + 1])
                yield
            for t in range(TILES):
                for c in range(FF_CHUNKS):
                    m = pe.do(T.matmul, [h], q1[:, t * P:(t + 1) * P], lhsT=L.eh[:, c, t * P:(t + 1) * P],
                              rhs=e_w2[:, c, :], start=(c == 0), stop=(c == FF_CHUNKS - 1))
            yield
            bc = [P, TILES, DIM]
            m = dve.do(V.tensor_tensor, [m], out=L.r, in0=q1.rearrange("p (t n) -> p t n", t=TILES),
                       in1=e_b2[:].unsqueeze(1).to_broadcast(bc), op=ALU.add)
            L.q_free = L.t_free = [m, h]
            m = dve.do(V.tensor_tensor, [m], out=L.r, in0=L.r, in1=L.xn[:], op=ALU.add)
            yield from layer_norm(L, L.r, L.r, [m])
            m = dve.do(V.tensor_tensor, [L.normed], out=L.r, in0=L.r, in1=gamma[:].unsqueeze(1).to_broadcast(bc),
                       op=ALU.mult)
            m = dve.do(V.tensor_tensor, [m], out=L.r, in0=L.r, in1=beta[:].unsqueeze(1).to_broadcast(bc),
                       op=ALU.add)
            m = dve.do(V.scalar_tensor_tensor, [m], out=L.x[:], in0=L.r, scalar=0.5, in1=L.x[:],
                       op0=ALU.mult, op1=ALU.add)
            L.x_done = [m]
            yield

        def silu_of(src, e, dst, after):
            m = act.do(A.activation, after, e, src, ACT.Exp, scale=-1.0)
            m = dve.do(V.tensor_scalar, [m], out=e, in0=e, scalar1=1.0, scalar2=None, op0=ALU.add)
            m = dve.do(V.reciprocal, [m], e, e)
            return dve.do(V.tensor_tensor, [m], out=dst, in0=src, in1=e, op=ALU.mult)

        def mamba(L):
            q0, q1, t0, t1 = L.q[:, 0, :], L.q[:, 1, :], L.t[:, 0, :], L.t[:, 1, :]
            yield from layer_norm(L, L.x, L.xn, L.x_done)
            m = to_features(L, L.xn, q0, [L.normed] + L.q_free)
            xT = act.do(A.activation, [m], L.hT[:], q0, ACT.Copy)
            z = pool.do(G.memset, L.x_done, L.xc[:, :, 0:D_CONV - 1], 0.0)
            pool.do(G.memset, [], L.dA[0][:, :, 0:1], 0.0)
            z0 = pool.do(G.memset, [], L.dA[1][:, :, 0:1], 0.0)
            yield
            for c, bank in enumerate((q0, q1, t0, t1)):
                m = pe.do(T.matmul, [xT] + L.q_free + L.t_free, bank, lhsT=W_in[:, c * P:(c + 1) * P], rhs=L.hT[:],
                          start=True, stop=True)
                if c == 1:
                    xc_mm = m
            xc = act.do(A.activation, [xc_mm, z], L.xc[:, :, D_CONV - 1:], L.q[:, :, :], ACT.Copy)
            yield
            gate = silu_of(L.t[:, :, :], L.tmp, L.gate, [m])
            yield
            conv = [xc, z]
            for j in range(D_CONV):
                nxt = []
                for c in range(CHUNKS):
                    tap = L.xc[:, c, j:j + SEQ]
                    if j == 0:
                        nxt.append(dve.do(V.tensor_scalar, conv, out=L.dt[:, c, :], in0=tap, scalar1=conv_w[:, c, 0:1],
                                          scalar2=conv_b[:, c:c + 1], op0=ALU.mult, op1=ALU.add))
                    else:
                        nxt.append(dve.do(V.scalar_tensor_tensor, conv[c:c + 1], out=L.dt[:, c, :], in0=tap,
                                          scalar=conv_w[:, c, j:j + 1], in1=L.dt[:, c, :],
                                          op0=ALU.mult, op1=ALU.add))
                conv = nxt
                yield
            xs = silu_of(L.dt, L.tmp, L.xs, conv + [gate])
            yield
            for c in range(CHUNKS):
                m1 = pe.do(T.matmul, [xs, xc], q0[0:DT_RANK, :], lhsT=W_x[:, c, 0:DT_RANK], rhs=L.xs[:, c, :],
                           start=(c == 0), stop=(c == CHUNKS - 1))
            for c in range(CHUNKS):
                m2 = pe.do(T.matmul, [xc], q1[0:32, :], lhsT=W_x[:, c, DT_RANK:DT_RANK + 32], rhs=L.xs[:, c, :],
                           start=(c == 0), stop=(c == CHUNKS - 1))
            dt_r = act.do(A.activation, [m1], L.hT[0:DT_RANK, :], q0[0:DT_RANK, :], ACT.Copy)
            rest = L.h[0].rearrange("p c n -> p (c n)")[0:32, 0:SEQ]
            mid = L.h[1].rearrange("p c n -> p (c n)").bitcast(BF16)[0:32, 0:SEQ]
            m = act.do(A.activation, [m2], L.bc3[0:32, :], q1[0:32, :], ACT.Copy)
            m = dve.do(V.tensor_tensor, [m], out=rest, in0=q1[0:32, :], in1=L.bc3[0:32, :], op=ALU.subtract)
            q1_free = m
            m = dve.do(V.tensor_copy, [m], mid, rest)
            m = dve.do(V.tensor_copy, [m], L.bc3[32:64, :], mid)
            split = dve.do(V.tensor_tensor, [], out=L.bc3[64:96, :], in0=rest, in1=mid, op=ALU.subtract)
            yield
            for c, bank in enumerate((t0, t1)):
                m = pe.do(T.matmul, [dt_r, gate], bank, lhsT=W_dt[:, c * P:(c + 1) * P], rhs=L.hT[0:DT_RANK, :],
                          start=True, stop=True)
            for c in range(CHUNKS):
                a = act.do(A.activation, [m, xs], L.tmp[:, c, :], L.t[:, c, :], ACT.Abs, bias=b_dt[:, c:c + 1])
            a = act.do(A.activation, [a], L.tmp, L.tmp, ACT.Exp, scale=-1.0)
            a = act.do(A.activation, [a], L.tmp, L.tmp, ACT.Ln, bias=1.0)
            for c in range(CHUNKS):
                r = dve.do(V.tensor_scalar, [m, a], out=L.dt[:, c, :], in0=L.t[:, c, :], scalar1=b_dt[:, c:c + 1],
                           scalar2=0.0, op0=ALU.add, op1=ALU.max)
            dt = dve.do(V.tensor_tensor, [r, a], out=L.dt, in0=L.dt, in1=L.tmp, op=ALU.add)
            dtx = dve.do(V.tensor_tensor, [dt], out=L.dtx, in0=L.dt, in1=L.xs, op=ALU.mult)
            yield
            both = [P, CHUNKS, SEQ]
            flat = lambda ap: ap.rearrange("p c n -> p (c n)")
            scanned, multiplied, summed = [None, None], [None, None], [None, None]
            b_free, c_free = [dt_r], [q1_free]
            for n in range(D_STATE):
                i = n % 2
                old = lambda marks: [marks[i]] if marks[i] else []
                bb = pe.do(T.matmul, [split] + b_free, q0, lhsT=spread[:, n, :], rhs=L.bc3[:], start=True, stop=True)
                cb = pe.do(T.matmul, c_free, q1, lhsT=spread[:, D_STATE + n, :], rhs=L.bc3[:], start=True, stop=True)
                for c in range(CHUNKS):
                    dA = act.do(A.activation, [dt, z0] + old(scanned), L.dA[i][:, c, 1:], L.dt[:, c, 1:], ACT.Exp,
                                scale=negA[:, c, n:n + 1])
                cs = act.do(A.activation, [cb] + old(multiplied), L.Cs[i], q1, ACT.Copy)
                c_free = [cs]
                m = dve.do(V.tensor_tensor, [bb, dtx], out=L.dBx, in0=q0.unsqueeze(1).to_broadcast(both),
                           in1=L.dtx, op=ALU.mult)
                b_free = [m]
                sc = dve.do(V.tensor_tensor_scan, [m, dA] + old(multiplied), out=flat(L.h[i]), data0=flat(L.dA[i]),
                            data1=flat(L.dBx), initial=0.0, op0=ALU.mult, op1=ALU.add)
                scanned[i] = sc
                hc = pool.do(G.tensor_tensor, [sc, cs] + old(summed), out=L.hC[i], in0=L.h[i],
                             in1=L.Cs[i].unsqueeze(1).to_broadcast(both), op=ALU.mult)
                multiplied[i] = hc
                for c in range(CHUNKS):
                    sm = pe.do(T.matmul, [hc, dt], L.t[:, c, :], lhsT=ident[:], rhs=L.hC[i][:, c, :],
                               start=(n == 0), stop=(n == D_STATE - 1))
                summed[i] = sm
                yield
            for c in range(CHUNKS):
                m = dve.do(V.scalar_tensor_tensor, [sm], out=L.xs[:, c, :], in0=L.xs[:, c, :],
                           scalar=skipD[:, c:c + 1], in1=L.t[:, c, :], op0=ALU.mult, op1=ALU.add)
            m = dve.do(V.tensor_tensor, [m], out=L.xs, in0=L.xs, in1=L.gate, op=ALU.mult)
            yield
            for t in range(TILES):
                for c in range(CHUNKS):
                    p = pe.do(T.matmul, [m] + b_free, q0[:, t * P:(t + 1) * P], lhsT=L.xs[:, c, t * P:(t + 1) * P],
                              rhs=W_out[:, c, :], start=(c == 0), stop=(c == CHUNKS - 1))
            m = dve.do(V.tensor_tensor, [p], out=L.x[:], in0=q0.rearrange("p (t n) -> p t n", t=TILES),
                       in1=L.x[:], op=ALU.add)
            L.x_done = [m]
            L.q_free = L.t_free = [m, cs]
            yield

        def lane_program(i):
            L = lanes[i]
            L.q_free = L.t_free = []
            stored = []
            for b in range(i, BATCH, LANES):
                if b >= LANES:
                    L.x_here = sp.dma(L.x_in, stored, L.x[:], x_dram[b])
                L.x_done = [L.x_here] + stored
                yield from macaron_transformer(L)
                yield from alibi_attention(L)
                yield from macaron_transformer(L)
                yield from expert_ffn(L)
                yield from mamba(L)
                yield from expert_ffn(L)
                stored = [sp.dma(L.x_out, L.x_done, out_dram[b], L.x[:])]
            L.stored = stored

        a, b = lane_program(0), lane_program(1)
        for _ in range(HEAD_START):
            next(a)
        for _ in weave(a, b):
            pass
        sp.wait([m for L in lanes for m in L.stored])

        block = ctx.enter_context(nc.Block())

        @block.sync
        def _(eng):
            sp.play(eng)

        @block.tensor
        def _(eng):
            pe.play(eng)

        @block.vector
        def _(eng):
            dve.play(eng)

        @block.scalar
        def _(eng):
            act.play(eng)

        @block.gpsimd
        def _(eng):
            pool.play(eng)


HEAD_START = 130

_INS = ["L0_attn_x", "L0_attn_W_qk", "L0_attn_alibi_slope", "L0_ffn_wqkv", "L0_ffn_q_scale", "L0_ffn_k_scale",
        "L0_ffn_wo", "L0_ffn_w1", "L0_ffn_w2", "L0_ffn_b2",
        "L1_attn_W_in", "L1_attn_W_x", "L1_attn_W_dt", "L1_attn_W_out", "L1_ffn_w1", "L1_ffn_w2", "L1_ffn_b2",
        "L1_ffn_gamma", "L1_ffn_beta"]


def kernel(**inputs):
    import concourse.bacc as bacc
    from concourse.bass_utils import run_bass_kernel_spmd

    nc = bacc.Bacc("TRN2", target_bir_lowering=False, num_devices=1)
    arrays = {name: np.ascontiguousarray(inputs[name]) for name in _INS}
    arrays["WvT"] = np.ascontiguousarray(np.asarray(inputs["L0_attn_W_v"]).T)
    arrays["columns"] = parameter_columns(inputs)
    arrays.update(constant_tables())
    d = {n: nc.dram_tensor(f"in_{n}", a.shape, mybir.dt.from_np(a.dtype), kind="ExternalInput").ap()
         for n, a in arrays.items()}
    out = nc.dram_tensor("out_0", (BATCH, SEQ, DIM), F32, kind="ExternalOutput").ap()
    macaron_kernel(nc, d, out)
    r = run_bass_kernel_spmd(nc, [{f"in_{n}": a for n, a in arrays.items()}], core_ids=[0])
    return r.results[0]["out_0"]
```

```python
import numpy as np
import concourse.bass as bass
from concourse import mybir
from contextlib import ExitStack

F32 = mybir.dt.float32
BF16 = mybir.dt.bfloat16
ALU = mybir.AluOpType
ACT = mybir.ActivationFunctionType
AX = mybir.AxisListType

P = 128
BATCH, SEQ, DIM = 8, 512, 128
TILES = SEQ // P
DEPTH, HEADS, HEAD = 2, 8, 64
INNER = HEADS * HEAD
WINDOW = 64
HID = int(DIM * 4 * 2 / 3)
HID_CHUNKS = [(c, min(P, HID - c)) for c in range(0, HID, P)]
PAIRS = INNER // P
QK_SCALE = 8.0
D_INNER, D_STATE, D_CONV, DT_RANK = 256, 16, 4, 64
CHUNKS = D_INNER // P
FF = 512
FF_CHUNKS = FF // P
LN_EPS = 1e-5
MASKED = -1e30
LANES = 4
STARTS = [0.0, 20e3, 40e3, 60e3]
WORK = 7700
BANK = 512


WIDTHS = {"ln": DEPTH * 2, "b1": DEPTH * 2 * 3, "e_b1": FF_CHUNKS, "conv_b": CHUNKS, "b_dt": CHUNKS, "D": CHUNKS,
          "A_log": CHUNKS * D_STATE, "conv_w": CHUNKS * D_CONV}
COLUMNS, COLUMNS_WIDTH = {}, 0
for _name, _width in WIDTHS.items():
    COLUMNS[_name] = (COLUMNS_WIDTH, _width)
    COLUMNS_WIDTH += _width


def parameter_columns(inputs):
    a = {n: np.asarray(inputs[n]) for n in inputs}
    ln = np.stack([a["L0_ffn_ln_g"], a["L0_ffn_ln_b"]], axis=1)
    b1 = a["L0_ffn_b1"].reshape(DEPTH, 2, HID)
    b1 = np.pad(b1, ((0, 0), (0, 0), (0, 3 * P - HID))).reshape(DEPTH, 2, 3, P)

    def by_chunk(v):
        return v.reshape(v.shape[0] // P, P, -1).transpose(1, 0, 2).reshape(P, -1)

    parts = {"ln": ln.transpose(2, 0, 1).reshape(P, -1), "b1": b1.transpose(3, 0, 1, 2).reshape(P, -1),
             "e_b1": by_chunk(a["L1_ffn_b1"][0]), "conv_b": by_chunk(a["L1_attn_conv_b"]),
             "b_dt": by_chunk(a["L1_attn_b_dt"]), "D": by_chunk(a["L1_attn_D"]),
             "A_log": by_chunk(a["L1_attn_A_log"]), "conv_w": by_chunk(a["L1_attn_conv_w"])}
    return np.ascontiguousarray(np.concatenate([parts[n] for n in WIDTHS], axis=1))


def constant_tables():
    f = np.float32
    half = np.arange(0, HEAD, 2, dtype=f)
    inv_freq = f(1.0) / (f(10000.0) ** (half / f(HEAD)))
    t = np.arange(SEQ, dtype=f)
    freqs = t[:, None] * inv_freq[None, :]
    freqs = np.concatenate([freqs, freqs], axis=-1)
    base = (half + f(0.4 * HEAD)) / f(1.4 * HEAD)
    power = (t - SEQ // 2) / f(WINDOW // 2)
    scale = base[None, :] ** power[:, None]
    scale = np.concatenate([scale, scale], axis=-1).astype(f)
    cos, sin = np.cos(freqs).astype(f), np.sin(freqs).astype(f)
    sign = np.concatenate([-np.ones(HEAD // 2, f), np.ones(HEAD // 2, f)])
    rotary = np.stack([cos * scale, cos / scale, sin * scale * sign, sin / scale * sign])
    rotary = rotary.reshape(2, 2, TILES, P, HEAD).transpose(3, 0, 2, 1, 4)

    row, col = np.arange(P)[:, None], np.arange(P)[None, :]
    even = row < WINDOW
    key = np.where(even & (col >= WINDOW), col - P, col)
    seen = (key <= row) & (row <= key + WINDOW)
    first = seen & (key >= 0)
    local = np.stack([np.where(m, 0.0, MASKED) for m in (first, seen)])
    local = np.tile(local[:, :, None, :], (1, 1, 4, 1)).transpose(1, 0, 2, 3)

    rel = (np.arange(SEQ)[None, :] - (SEQ - P) - row).astype(f)
    causal = np.where(rel <= 0, 0.0, MASKED).astype(f)

    bf = mybir.dt.np(BF16)
    return {
        "c_rotary": np.ascontiguousarray(rotary, f),
        "c_local": np.ascontiguousarray(local.astype(bf)),
        "c_rel": rel,
        "c_causal": causal,
        "c_ident": np.eye(P, dtype=f),
        "c_ident16": np.eye(P, dtype=f).astype(bf),
    }


class Clock:
    now = 0.0


class Engine:

    def __init__(self, sem, fixed, per_element, latency=0.0):
        self.sem, self.count, self.items, self.seen = sem, 0, [], {}
        self.fixed, self.per_element, self.latency, self.free_at = fixed, per_element, latency, 0.0

    def wait(self, after):
        for sem, value, at in after:
            self.free_at = max(self.free_at, at)
            if self.seen.get(id(sem), 0) < value:
                self.seen[id(sem)] = value
                self.items.append(("wait", sem, value))

    def spend(self, args, kw):
        sizes = [a.free_size() for a in list(args) + list(kw.values()) if isinstance(a, bass.AP)]
        elements = kw["rhs"].free_size() * (1 if kw["rhs"].dtype == BF16 else 4) if "rhs" in kw else max(sizes)
        self.free_at += self.fixed + self.per_element * elements
        Clock.now = self.free_at + self.latency
        return Clock.now

    def do(self, method, after, *args, **kw):
        self.wait(after)
        self.count += 1
        self.items.append(("do", method, args, kw, self.sem, 1))
        return (self.sem, self.count, self.spend(args, kw))

    def quiet(self, method, after, *args, **kw):
        self.wait(after)
        self.spend(args, kw)
        self.items.append(("do", method, args, kw, None, 0))

    def dma(self, counter, after, out, in_):
        self.wait(after)
        self.items.append(("do", self.dma_method, (out, in_), {}, counter.sem, 16))
        counter.value += 16
        self.free_at += 60.0
        Clock.now = self.free_at + 2200.0
        return (counter.sem, counter.value, Clock.now)

    def play(self, eng):
        for item in self.items:
            if item[0] == "wait":
                eng.wait_ge(item[1], item[2])
            else:
                _, method, args, kw, sem, inc = item
                ins = method(*args, **kw)
                if sem is not None:
                    ins.then_inc(sem, inc)


class DmaCount:

    def __init__(self, sem):
        self.sem, self.value = sem, 0


def issue(programs, starts):
    ready = dict(enumerate(starts))
    while ready:
        i = min(ready, key=lambda k: ready[k])
        try:
            next(programs[i])
            ready[i] = max(ready[i], Clock.now)
        except StopIteration:
            del ready[i]


def macaron_kernel(nc, d, out_d):
    ctx = ExitStack()
    with ctx:
        def sb(name, shape, dt=F32):
            return ctx.enter_context(nc.sbuf_tensor(name, shape, dt))

        def sem(name):
            return ctx.enter_context(nc.semaphore(name))

        pe = Engine(sem("pe_done"), 10.0, 0.42, 250.0)
        dve = Engine(sem("dve_done"), 65.0, 1.04, 100.0)
        act = Engine(sem("act_done"), 190.0, 0.83, 60.0)
        pool = Engine(sem("pool_done"), 100.0, 2.2, 100.0)
        sp = Engine(sem("sp_done"), 60.0, 0.0)
        sp.dma_method = nc.sync.dma_start
        V, A, G, T = nc.vector, nc.scalar, nc.gpsimd, nc.tensor

        ident = sb("ident", [P, P])
        ident16 = sb("ident16", [P, P], BF16)
        local_mask = sb("local_mask", [P, 2, 4 * P], BF16)
        alibi = sb("alibi", [P, SEQ])
        slope = sb("slope", [P, 1])
        rot = [sb(f"rot{l}", [P, 2, TILES, 2, HEAD]) for l in range(DEPTH)]
        qk_gain = sb("qk_gain", [P, DEPTH, 2, HEAD])
        wqkv = sb("wqkv", [P, DEPTH, 3 * INNER])
        wo = sb("wo", [P, DEPTH, PAIRS, DIM])
        columns = sb("columns", [P, COLUMNS_WIDTH])
        col = {n: columns[:, at:at + w] for n, (at, w) in COLUMNS.items()}
        lnT = col["ln"].rearrange("p (l a) -> p l a", l=DEPTH)
        w1 = sb("w1", [P, DEPTH, 2 * HID])
        b1T = col["b1"].rearrange("p (l a c) -> p l a c", l=DEPTH, a=2)
        w2 = sb("w2", [P, DEPTH, 3, DIM])
        Wqk = sb("Wqk", [P, DIM])
        WvT = sb("WvT", [P, DIM])
        W_in = sb("W_in", [P, 2 * D_INNER])
        conv_w = col["conv_w"].rearrange("p (c j) -> p c j", c=CHUNKS)
        conv_b = col["conv_b"]
        W_x = sb("W_x", [P, CHUNKS, DT_RANK + 2 * D_STATE])
        W_dt = sb("W_dt", [DT_RANK, D_INNER])
        b_dt = col["b_dt"]
        negA = sb("negA", [P, CHUNKS, D_STATE])
        skipD = col["D"]
        W_out = sb("W_out", [P, CHUNKS, DIM])
        e_w1 = sb("e_w1", [P, FF])
        e_b1 = col["e_b1"]
        e_w2 = sb("e_w2", [P, FF_CHUNKS, DIM])
        e_b2 = sb("e_b2", [P, DIM])
        gamma = sb("gamma", [P, DIM])
        beta = sb("beta", [P, DIM])
        neg_half = sb("neg_half", [P, 16])

        loaded = DmaCount(sem("weights_loaded"))

        def load(dst, src):
            sp.dma(loaded, [], dst, src)

        class Lane:
            pass

        def new_lane(i):
            L = Lane()
            L.x = sb(f"x{i}", [P, TILES, DIM])
            spare = sb(f"spare{i}", [P, 2, TILES, DIM])
            L.y, L.xn = spare[:, 0], spare[:, 1]
            L.hT = sb(f"hT{i}", [P, SEQ])
            L.stats = sb(f"stats{i}", [P, TILES, 6])
            L.mv = sb(f"mv{i}", [P, TILES, 2])
            L.rstd = sb(f"rstd{i}", [P, TILES])
            L.ss = sb(f"ss{i}", [P, 16])
            L.rn = sb(f"rn{i}", [P, 16])
            L.mx = sb(f"mx{i}", [P, HEADS])
            L.rs = sb(f"rs{i}", [P, HEADS])
            L.work = sb(f"work{i}", [P, WORK])
            L.banks = ctx.enter_context(nc.psum_tensor(f"banks{i}", [P, 2, BANK], F32))
            L.x_in = DmaCount(sem(f"x_in{i}"))
            L.x_out = DmaCount(sem(f"x_out{i}"))
            L.shift_in = DmaCount(sem(f"shift_in{i}"))
            L.v_in = DmaCount(sem(f"v_in{i}"))
            L.rows_out = DmaCount(sem(f"rows_out{i}"))
            L.rows_in = [DmaCount(sem(f"rows_in{i}_{k}")) for k in range(2)]
            L.rows_dram = nc.dram_tensor(f"bc_rows{i}", (2 * D_STATE, SEQ), F32, kind="Internal").ap()

            at = [0]

            def cut(*shape):
                n = int(np.prod(shape))
                ap = L.work[:, at[0]:at[0] + n]
                at[0] += n
                assert at[0] <= WORK
                if len(shape) == 2:
                    ap = ap.rearrange("p (a b) -> p a b", a=shape[0])
                elif len(shape) == 3:
                    ap = ap.rearrange("p (a b c) -> p a b c", a=shape[0], b=shape[1])
                return ap

            L.sq = L.ts = cut(16, HEAD)
            L.tq = cut(16, HEAD)
            L.tc = cut(16, HEAD)
            L.prob = L.tq.rearrange("p (a b) d -> p a (b d)", b=2)
            L.probT = L.tc.rearrange("p (a b) d -> p a (b d)", b=2)
            L.o, L.oT = L.prob[:, 0:4, :], L.probT[:, 0:4, :]
            L.qT = cut(PAIRS, P)
            L.kT = [cut(PAIRS, P) for _ in range(2)]
            L.V = [cut(HEADS, HEAD + 1) for _ in range(2)]
            L.Vc = cut(HEADS, HEAD + 1)
            at[0] = 0
            L.hid = cut(3, SEQ)
            L.gelu = [cut(SEQ) for _ in range(2)]
            at[0] = 0
            L.uT = cut(SEQ)
            L.va = cut(TILES, DIM)
            L.ap = cut(SEQ)
            L.apT = cut(TILES, P)
            at[0] = 0
            L.gate = spare[:].rearrange("p c t n -> p c (t n)")
            L.xc = cut(CHUNKS, SEQ + D_CONV - 1)
            L.dBx = L.work[:, 0:CHUNKS * SEQ].rearrange("p (c n) -> p c n", c=CHUNKS)
            L.xs = cut(CHUNKS, SEQ)
            L.dt = cut(CHUNKS, SEQ)
            L.dtx = cut(CHUNKS, SEQ)
            L.dA = L.tmp = cut(CHUNKS, SEQ)
            L.h = cut(CHUNKS, SEQ)
            L.bcs = L.h.rearrange("p c n -> p (c n)")[0:2 * D_STATE, 0:SEQ]
            L.Bs = [cut(SEQ) for _ in range(2)]
            L.Cs = [cut(SEQ), L.hT[:]]
            at[0] = 0
            L.eh = cut(FF_CHUNKS, SEQ)
            L.r = L.y
            return L

        lanes = [new_lane(i) for i in range(LANES)]
        rot_base = lanes[-1].work[:, 0:1024].rearrange("p (a t b d) -> p a t b d", a=2, t=TILES, b=2)
        rel = lanes[-1].work[:, 1024:1024 + SEQ]
        x_dram = d["L0_attn_x"].rearrange("b (t p) d -> b p t d", p=P)
        out_dram = out_d.rearrange("b (t p) d -> b p t d", p=P)

        for i, L in enumerate(lanes):
            L.x_here = sp.dma(L.x_in, [], L.x[:], x_dram[i])
        load(ident[:], d["c_ident"])
        load(ident16[:], d["c_ident16"])
        load(wqkv[:], d["L0_ffn_wqkv"].rearrange("l k n -> k l n"))
        load(rot_base, d["c_rotary"])
        for l in range(DEPTH):
            load(qk_gain[:, l, 0, :], d["L0_ffn_q_scale"][l].partition_broadcast(P))
            load(qk_gain[:, l, 1, :], d["L0_ffn_k_scale"][l].partition_broadcast(P))
        load(local_mask[:], d["c_local"].rearrange("p a b c -> p a (b c)"))
        load(wo[:], d["L0_ffn_wo"].rearrange("l (c p) n -> p l c n", p=P))
        load(w1[:], d["L0_ffn_w1"].rearrange("l k n -> k l n"))
        for c, (c0, n) in enumerate(HID_CHUNKS):
            for l in range(DEPTH):
                load(w2[0:n, l, c, :], d["L0_ffn_w2"][l, c0:c0 + n, :])
        last_rows = HID_CHUNKS[-1][1]
        for l in range(DEPTH):
            load(w2[last_rows:last_rows + 1, l, 2, :], d["L0_ffn_b2"][l:l + 1, :])
        load(columns[:], d["columns"])
        load(Wqk[:], d["L0_attn_W_qk"])
        load(WvT[:], d["WvT"])
        load(slope[:], d["L0_attn_alibi_slope"].partition_broadcast(P))
        load(rel, d["c_rel"])
        load(alibi[:], d["c_causal"])
        load(e_w1[:], d["L1_ffn_w1"][0])
        load(e_w2[:], d["L1_ffn_w2"][0].rearrange("(c p) n -> p c n", p=P))
        load(e_b2[:], d["L1_ffn_b2"][0].partition_broadcast(P))
        load(gamma[:], d["L1_ffn_gamma"].partition_broadcast(P))
        load(beta[:], d["L1_ffn_beta"].partition_broadcast(P))
        load(W_in[:], d["L1_attn_W_in"])
        load(W_x[:], d["L1_attn_W_x"].rearrange("(c p) n -> p c n", p=P))
        load(W_dt[:], d["L1_attn_W_dt"])
        load(W_out[:], d["L1_attn_W_out"].rearrange("(c p) n -> p c n", p=P))
        weights = (loaded.sem, loaded.value, 0.0)

        H2 = HEAD // 2
        const = pool.do(G.memset, [], neg_half[:], -0.5)
        for l in range(DEPTH):
            g = qk_gain[:, l].unsqueeze(1)
            full = [P, TILES, 2, HEAD]
            half = [P, TILES, 2, H2]
            dve.do(V.tensor_tensor, [weights], out=rot[l][:, 0], in0=rot_base[:, 0],
                   in1=g.to_broadcast(full), op=ALU.mult)
            dve.do(V.tensor_tensor, [], out=rot[l][:, 1, :, :, 0:H2], in0=rot_base[:, 1, :, :, 0:H2],
                   in1=g[:, :, :, H2:HEAD].to_broadcast(half), op=ALU.mult)
            dve.do(V.tensor_tensor, [], out=rot[l][:, 1, :, :, H2:HEAD], in0=rot_base[:, 1, :, :, H2:HEAD],
                   in1=g[:, :, :, 0:H2].to_broadcast(half), op=ALU.mult)
        dve.do(V.scalar_tensor_tensor, [], out=alibi[:], in0=rel, scalar=slope[:, 0:1],
               in1=alibi[:], op0=ALU.mult, op1=ALU.add)
        A_log = col["A_log"].rearrange("p (c n) -> p c n", c=CHUNKS)
        exp_A = act.do(A.activation, [weights], negA[:], A_log, ACT.Exp)
        tables = dve.do(V.tensor_scalar, [exp_A], out=negA[:], in0=negA[:], scalar1=-1.0, scalar2=None,
                        op0=ALU.mult)
        ready = [weights, tables, const]


        def layer_norm(L, src, dst, after):
            for t in range(TILES):
                m = dve.do(V.bn_stats, after, L.stats[:, t, :], src[:, t, :])
            for t in range(TILES):
                m = dve.do(V.bn_aggr, [m], L.mv[:, t, :], L.stats[:, t, :])
            yield
            m = dve.do(V.tensor_scalar, [m], out=L.rstd[:], in0=L.mv[:, :, 1], scalar1=LN_EPS, scalar2=None,
                       op0=ALU.add)
            m = pool.do(G.tensor_tensor, [m, const], out=L.rstd[:], in0=L.rstd[:], in1=neg_half[:, 0:TILES],
                        op=ALU.pow)
            yield
            for t in range(TILES):
                m = dve.do(V.tensor_scalar, [m], out=dst[:, t, :], in0=src[:, t, :],
                           scalar1=L.mv[:, t, 0:1], scalar2=L.rstd[:, t:t + 1],
                           op0=ALU.subtract, op1=ALU.mult)
            L.normed = m
            yield

        def to_features(L, src, bank, after):
            for t in range(TILES):
                m = pe.do(T.transpose, after, bank[:, t * P:(t + 1) * P], src[:, t, :], ident[:])
            return m

        def project(L, l, t, after):
            hT = L.hT[:, t * P:(t + 1) * P]
            b0, b1 = L.banks[:, 0, :], L.banks[:, 1, :]
            pe.quiet(T.matmul, after + L.free, b0, lhsT=hT, rhs=wqkv[:, l, 0:INNER], start=True, stop=True)
            qk = pe.do(T.matmul, [], b1, lhsT=hT, rhs=wqkv[:, l, INNER:2 * INNER], start=True, stop=True)
            yield
            qk_view = L.banks[:, :, :].rearrange("p a (h d) -> p (a h) d", d=HEAD)
            squared = act.do(A.activation, [qk] + L.free, L.sq, qk_view, ACT.Square)
            yield
            m = dve.do(V.tensor_reduce, [squared], out=L.ss[:], in_=L.sq, axis=AX.X, op=ALU.add)
            m = dve.do(V.tensor_scalar, [m], out=L.ss[:], in0=L.ss[:], scalar1=1e-24, scalar2=None, op0=ALU.max)
            yield
            norm = pool.do(G.tensor_tensor, [m, const], out=L.rn[:], in0=L.ss[:], in1=neg_half[:], op=ALU.pow)
            Clock.now += 2500.0
            yield
            unit = dve.do(V.tensor_tensor, [norm, qk], out=L.tq, in0=qk_view,
                          in1=L.rn[:].unsqueeze(2).to_broadcast([P, 16, HEAD]), op=ALU.mult)
            yield
            v = pe.do(T.matmul, [unit], b0, lhsT=hT, rhs=wqkv[:, l, 2 * INNER:3 * INNER], start=True, stop=True)
            tq4 = L.tq.rearrange("p (a h) d -> p a h d", a=2)
            ts4 = L.ts.rearrange("p (a h) d -> p a h d", a=2)
            tc4 = L.tc.rearrange("p (a h) d -> p a h d", a=2)
            cos = rot[l][:, 0, t].unsqueeze(2)
            sin = rot[l][:, 1, t].unsqueeze(2)
            hb = [P, 2, HEADS, H2]
            dve.do(V.tensor_tensor, [unit], out=ts4[:, :, :, 0:H2], in0=tq4[:, :, :, H2:HEAD],
                   in1=sin[:, :, :, 0:H2].to_broadcast(hb), op=ALU.mult)
            sined = dve.do(V.tensor_tensor, [], out=ts4[:, :, :, H2:HEAD], in0=tq4[:, :, :, 0:H2],
                           in1=sin[:, :, :, H2:HEAD].to_broadcast(hb), op=ALU.mult)
            v_copied = act.do(A.activation, [v], L.V[t % 2][:, :, 0:HEAD],
                              b0.rearrange("p (h d) -> p h d", d=HEAD), ACT.Copy)
            v_dma = sp.dma(L.v_in, [v_copied], L.Vc[0:WINDOW], L.V[t % 2][0:WINDOW])
            if t > 0:
                v_dma = sp.dma(L.v_in, [], L.Vc[WINDOW:P], L.V[(t - 1) % 2][WINDOW:P])
            cosined = pool.do(G.tensor_tensor, [unit], out=tc4, in0=tq4,
                              in1=cos.to_broadcast([P, 2, HEADS, HEAD]), op=ALU.mult)
            yield
            tcf = L.tc.rearrange("p (c h) d -> p c (h d)", h=2)
            tsf = L.ts.rearrange("p (c h) d -> p c (h d)", h=2)
            for side, bank, wait in ((0, b1, [cosined, sined]), (1, b0, [v_copied])):
                for c in range(PAIRS):
                    dst = bank[:, c * P:(c + 1) * P]
                    pe.quiet(T.matmul, wait, dst, lhsT=tcf[:, side * PAIRS + c, :], rhs=ident[:],
                             is_transpose=True, start=True, stop=False)
                    m = pe.do(T.matmul, [], dst, lhsT=tsf[:, side * PAIRS + c, :], rhs=ident[:],
                              is_transpose=True, start=False, stop=True)
                if side == 0:
                    q_ready = m
            yield
            q_copied = act.do(A.activation, [q_ready], L.qT, b1.rearrange("p (c n) -> p c n", c=PAIRS), ACT.Copy)
            k_copied = act.do(A.activation, [m], L.kT[t % 2], b0.rearrange("p (c n) -> p c n", c=PAIRS), ACT.Copy)
            L.qk_here = [q_copied, k_copied]
            L.v_here = [v_copied, v_dma]
            yield

        def local_attention(L, l, t):
            b0, b1 = L.banks[:, 0, :], L.banks[:, 1, :]
            mask = local_mask[:, min(t, 1), :]
            pe.quiet(T.matmul, L.qk_here, b0, lhsT=ident16[:], rhs=mask, start=True, stop=False,
                     skip_group_check=True)
            pe.quiet(T.matmul, [], b1, lhsT=ident16[:], rhs=mask, start=True, stop=False, skip_group_check=True)
            for h in range(HEADS):
                rows = slice((h % 2) * HEAD, (h % 2 + 1) * HEAD)
                bank = L.banks[:, h % 2, :]
                c0 = (h // 2) * P
                q = L.qT[rows, h // 2, :]
                k = L.kT[t % 2][rows, h // 2, :]
                before = L.kT[(t - 1) % 2][rows, h // 2, WINDOW:P] if t > 0 else k[:, 0:WINDOW]
                pe.quiet(T.matmul, [], bank[:, c0:c0 + WINDOW], lhsT=q, rhs=k[:, 0:WINDOW],
                         start=False, stop=True, skip_group_check=True)
                pe.quiet(T.matmul, [], bank[0:WINDOW, c0 + WINDOW:c0 + P], lhsT=q[:, 0:WINDOW],
                         rhs=before, start=False, stop=True, skip_group_check=True)
                scored = pe.do(T.matmul, [], bank[WINDOW:P, c0 + WINDOW:c0 + P], lhsT=q[:, WINDOW:P],
                               rhs=k[:, WINDOW:P], start=False, stop=True, skip_group_check=True)
            yield
            s = L.banks[:, :, :].rearrange("p a (j n) -> p (a j) n", n=P)
            m = dve.do(V.tensor_reduce, [scored], out=L.mx[:], in_=s, axis=AX.X, op=ALU.max)
            yield
            lowered = dve.do(V.tensor_tensor, [m], out=L.prob, in0=s,
                             in1=L.mx[:].unsqueeze(2).to_broadcast([P, 8, P]), op=ALU.subtract)
            yield
            raised = act.do(A.activation, [lowered], L.prob, L.prob, ACT.Exp, scale=QK_SCALE)
            yield
            for b in range(8):
                m = pe.do(T.transpose, [raised], L.banks[:, b // 4, (b % 4) * P:(b % 4 + 1) * P],
                          L.prob[:, b, :], ident[:])
            yield
            copied = act.do(A.activation, [m], L.probT, s, ACT.Copy)
            yield
            W1 = HEAD + 1
            for b in range(8):
                h = 2 * (b % 4) + b // 4
                dst = L.banks[:, b // 4, (b % 4) * W1:(b % 4 + 1) * W1]
                pe.quiet(T.matmul, [copied] + L.v_here, dst[0:WINDOW], lhsT=L.probT[:, b, 0:WINDOW],
                         rhs=L.Vc[:, h, :], start=True, stop=True)
                m = pe.do(T.matmul, [], dst[WINDOW:P], lhsT=L.probT[:, b, WINDOW:P],
                          rhs=L.V[t % 2][:, h, :], start=True, stop=True)
            yield
            o = L.banks[:, :, 0:4 * W1].rearrange("p a (j w) -> p a j w", w=W1)
            rs = L.rs[:].rearrange("p (a j) -> p a j", a=2)
            m = dve.do(V.reciprocal, [m], rs, o[:, :, :, HEAD])
            yield
            divided = dve.do(V.tensor_tensor, [m],
                             out=L.o.rearrange("p j (a d) -> p a j d", a=2), in0=o[:, :, :, 0:HEAD],
                             in1=rs.unsqueeze(3).to_broadcast([P, 2, 4, HEAD]), op=ALU.mult)
            yield
            for c in range(PAIRS):
                m = pe.do(T.transpose, [divided], b0[:, c * P:(c + 1) * P], L.o[:, c, :], ident[:])
            yield
            oT = act.do(A.activation, [m], L.oT, b0.rearrange("p (c n) -> p c n", c=PAIRS), ACT.Copy)
            yield
            for c in range(PAIRS):
                m = pe.do(T.matmul, [oT], b1[:, 0:DIM], lhsT=L.oT[:, c, :], rhs=wo[:, l, c, :],
                          start=(c == 0), stop=(c == PAIRS - 1))
            yield
            added = dve.do(V.tensor_tensor, [m], out=L.y[:, t, :], in0=b1[:, 0:DIM], in1=L.y[:, t, :], op=ALU.add)
            L.free = [added]
            yield

        def transformer_layer(L, l):
            b0, b1 = L.banks[:, 0, :], L.banks[:, 1, :]
            m = to_features(L, L.y, b0, L.free)
            a = act.do(A.activation, [m], L.hT[0:HEAD, :], b0[0:HEAD, :], ACT.Copy)
            b = act.do(A.activation, [], L.hT[HEAD:P, 1:SEQ], b0[HEAD:P, 0:SEQ - 1], ACT.Copy)
            z = dve.do(V.memset, L.free, L.hT[HEAD:P, 0:1], 0.0)
            zv = pool.do(G.memset, L.free, L.Vc, 0.0)
            L.free = [a, b, z, zv]
            yield
            for t in range(TILES):
                yield from project(L, l, t, [])
                yield from local_attention(L, l, t)
            sh = pool.do(G.tensor_copy, L.free, L.xn[:, :, 0:HEAD], L.y[:, :, 0:HEAD])
            z = pool.do(G.memset, [], L.xn[:, 0, HEAD:DIM], 0.0)
            sp.dma(L.shift_in, L.free + [z], L.xn[1:113, :, HEAD:DIM], L.y[0:112, :, HEAD:DIM])
            sp.dma(L.shift_in, [], L.xn[113:128, :, HEAD:DIM], L.y[112:127, :, HEAD:DIM])
            sd = sp.dma(L.shift_in, [], L.xn[0:1, 1:TILES, HEAD:DIM], L.y[127:128, 0:TILES - 1, HEAD:DIM])
            yield
            yield from layer_norm(L, L.xn, L.xn, [sh, sd])
            m = to_features(L, L.xn, b0, [L.normed])
            yield
            hT = act.do(A.activation, [m], L.hT[:], b0, ACT.Identity, bias=lnT[:, l, 1:2], scale=lnT[:, l, 0:1])
            ones = dve.do(V.memset, L.free, L.hid[HEAD:P, 2, :], 1.0)
            yield
            g_free, u_free = [], []
            for c, (c0, n) in enumerate(HID_CHUNKS):
                g = pe.do(T.matmul, [hT] + g_free, b1[0:n, :], lhsT=w1[:, l, HID + c0:HID + c0 + n], rhs=L.hT[:],
                          start=True, stop=True)
                u = pe.do(T.matmul, u_free, b0[0:n, :], lhsT=w1[:, l, c0:c0 + n], rhs=L.hT[:], start=True, stop=True)
                yield
                gelu_old = u_free if c == 2 else []
                g_free = [act.do(A.activation, [g] + gelu_old, L.gelu[c % 2][0:n, :], b1[0:n, :], ACT.Gelu,
                                 bias=b1T[0:n, l, 1, c:c + 1])]
                hd = dve.do(V.scalar_tensor_tensor, [u, g_free[0], ones], out=L.hid[0:n, c, :], in0=b0[0:n, :],
                            scalar=b1T[0:n, l, 0, c:c + 1], in1=L.gelu[c % 2][0:n, :],
                            op0=ALU.add, op1=ALU.mult)
                u_free = [hd]
                yield
            for t in range(TILES):
                for c, (c0, n) in enumerate(HID_CHUNKS):
                    k = n + 1 if c == 2 else n
                    m = pe.do(T.matmul, [hd], b1[:, t * P:(t + 1) * P], lhsT=L.hid[0:k, c, t * P:(t + 1) * P],
                              rhs=w2[0:k, l, c, :], start=(c == 0), stop=(c == 2))
            yield
            m = dve.do(V.tensor_tensor, [m], out=L.y, in0=b1.rearrange("p (t n) -> p t n", t=TILES),
                       in1=L.y, op=ALU.add)
            L.free = [m]
            yield

        def macaron_transformer(L):
            for v in L.V:
                ones = pool.do(G.memset, L.free + ready, v[:, :, HEAD:HEAD + 1], 1.0)
            yield from layer_norm(L, L.x[:], L.y, L.free)
            L.free = [L.normed, ones]
            for l in range(DEPTH):
                if l:
                    for v in L.V:
                        ones = pool.do(G.memset, L.free, v[:, :, HEAD:HEAD + 1], 1.0)
                    L.free = L.free + [ones]
                yield from transformer_layer(L, l)
            m = dve.do(V.scalar_tensor_tensor, L.free, out=L.x[:], in0=L.y, scalar=0.5, in1=L.x[:],
                       op0=ALU.mult, op1=ALU.add)
            L.free = [m]
            yield

        def alibi_attention(L):
            b0, b1 = L.banks[:, 0, :], L.banks[:, 1, :]
            yield from layer_norm(L, L.x[:], L.xn, L.free)
            m = to_features(L, L.xn, b0, [L.normed])
            yield
            xT = act.do(A.activation, [m], L.hT[:], b0, ACT.Copy)
            yield
            m = pe.do(T.matmul, [xT], b1, lhsT=Wqk[:], rhs=L.hT[:], start=True, stop=True)
            uT = act.do(A.activation, [m], L.uT, b1, ACT.Copy)
            for t in range(TILES):
                m = pe.do(T.matmul, [], b0[:, t * P:(t + 1) * P], lhsT=L.hT[:, t * P:(t + 1) * P], rhs=WvT[:],
                          start=True, stop=True)
            yield
            va = act.do(A.activation, [m], L.va, b0.rearrange("p (t n) -> p t n", t=TILES), ACT.Copy)
            yield
            scale = float(np.float32(1.0 / np.sqrt(DIM)))
            free = [va]
            for t in range(TILES):
                n = (t + 1) * P
                m = pe.do(T.matmul, [uT] + free, b0[:, 0:n], lhsT=L.uT[:, t * P:(t + 1) * P],
                          rhs=L.hT[:, 0:n], start=True, stop=True)
                yield
                sc = dve.do(V.scalar_tensor_tensor, [m], out=L.ap[:, 0:n], in0=b0[:, 0:n], scalar=scale,
                            in1=alibi[:, SEQ - n:SEQ], op0=ALU.mult, op1=ALU.add)
                m = dve.do(V.tensor_reduce, [sc], out=L.mx[:, 0:1], in_=L.ap[:, 0:n], axis=AX.X, op=ALU.max,
                           negate=True)
                yield
                ex = act.do(A.activation, [m], L.ap[:, 0:n], L.ap[:, 0:n], ACT.Exp,
                            bias=L.mx[:, 0:1], accum_out=L.rs[:, 0:1])
                yield
                for k in range(t + 1):
                    m = pe.do(T.transpose, [ex], b1[:, k * P:(k + 1) * P], L.ap[:, k * P:(k + 1) * P], ident[:])
                r = dve.do(V.reciprocal, [ex], L.rs[:, 1:2], L.rs[:, 0:1])
                yield
                pT = act.do(A.activation, [m], L.apT[:, 0:t + 1, :],
                            b1[:, 0:n].rearrange("p (t n) -> p t n", t=t + 1), ACT.Copy)
                yield
                for k in range(t + 1):
                    m = pe.do(T.matmul, [pT], b0[:, 0:DIM], lhsT=L.apT[:, k, :], rhs=L.va[:, k, :],
                              start=(k == 0), stop=(k == t))
                yield
                xd = dve.do(V.scalar_tensor_tensor, [m, r], out=L.x[:, t, :], in0=b0[:, 0:DIM],
                            scalar=L.rs[:, 1:2], in1=L.x[:, t, :], op0=ALU.mult, op1=ALU.add)
                free = [xd]
                yield
            L.free = [xd]

        def expert_ffn(L):
            banks = [L.banks[:, 1, :], L.banks[:, 0, :]]
            yield from layer_norm(L, L.x[:], L.xn, L.free)
            m = to_features(L, L.xn, banks[1], [L.normed])
            yield
            xT = act.do(A.activation, [m], L.hT[:], banks[1], ACT.Copy)
            yield
            done = [[], [xT]]
            for c in range(FF_CHUNKS):
                m = pe.do(T.matmul, [xT] + done[c % 2], banks[c % 2], lhsT=e_w1[:, c * P:(c + 1) * P],
                          rhs=L.hT[:], start=True, stop=True)
                yield
                h = act.do(A.activation, [m], L.eh[:, c, :], banks[c % 2], ACT.Relu, bias=e_b1[:, c:c + 1])
                done[c % 2] = [h]
            yield
            for t in range(TILES):
                for c in range(FF_CHUNKS):
                    m = pe.do(T.matmul, [h], banks[0][:, t * P:(t + 1) * P], lhsT=L.eh[:, c, t * P:(t + 1) * P],
                              rhs=e_w2[:, c, :], start=(c == 0), stop=(c == FF_CHUNKS - 1))
            yield
            bc = [P, TILES, DIM]
            m = dve.do(V.tensor_tensor, [m], out=L.r, in0=banks[0].rearrange("p (t n) -> p t n", t=TILES),
                       in1=e_b2[:].unsqueeze(1).to_broadcast(bc), op=ALU.add)
            m = dve.do(V.tensor_tensor, [m], out=L.r, in0=L.r, in1=L.xn, op=ALU.add)
            yield from layer_norm(L, L.r, L.r, [m])
            m = dve.do(V.tensor_tensor, [L.normed], out=L.r, in0=L.r, in1=gamma[:].unsqueeze(1).to_broadcast(bc),
                       op=ALU.mult)
            m = dve.do(V.tensor_tensor, [m], out=L.r, in0=L.r, in1=beta[:].unsqueeze(1).to_broadcast(bc),
                       op=ALU.add)
            m = dve.do(V.scalar_tensor_tensor, [m], out=L.x[:], in0=L.r, scalar=0.5, in1=L.x[:],
                       op0=ALU.mult, op1=ALU.add)
            L.free = [m]
            yield

        def silu(src, th, dst, after):
            m = act.do(A.activation, after, th, src, ACT.Tanh, scale=0.5)
            yield
            m = dve.do(V.tensor_scalar, [m], out=th, in0=th, scalar1=0.5, scalar2=0.5, op0=ALU.mult, op1=ALU.add)
            m = dve.do(V.tensor_tensor, [m], out=dst, in0=src, in1=th, op=ALU.mult)
            yield m

        def mamba(L):
            b0, b1 = L.banks[:, 0, :], L.banks[:, 1, :]
            both_banks = L.banks[:, :, :]
            yield from layer_norm(L, L.x[:], L.xn, L.free)
            m = to_features(L, L.xn, b0, [L.normed])
            z = pool.do(G.memset, L.free, L.xc[:, :, 0:D_CONV - 1], 0.0)
            yield
            xT = act.do(A.activation, [m], L.hT[:], b0, ACT.Copy)
            yield
            for c, bank in enumerate((b0, b1)):
                m = pe.do(T.matmul, [xT], bank, lhsT=W_in[:, c * P:(c + 1) * P], rhs=L.hT[:], start=True, stop=True)
            yield
            xc = act.do(A.activation, [m, z], L.xc[:, :, D_CONV - 1:], both_banks, ACT.Copy)
            yield
            for c, bank in enumerate((b0, b1)):
                m = pe.do(T.matmul, [xc], bank, lhsT=W_in[:, D_INNER + c * P:D_INNER + (c + 1) * P], rhs=L.hT[:],
                          start=True, stop=True)
            for gate in silu(both_banks, L.tmp, L.gate, [m]):
                yield
            conv = [xc, xc]
            for j in range(D_CONV):
                nxt = []
                for c in range(CHUNKS):
                    tap = L.xc[:, c, j:j + SEQ]
                    if j == 0:
                        nxt.append(dve.do(V.tensor_scalar, conv[c:c + 1], out=L.dt[:, c, :], in0=tap,
                                          scalar1=conv_w[:, c, 0:1], scalar2=conv_b[:, c:c + 1],
                                          op0=ALU.mult, op1=ALU.add))
                    else:
                        nxt.append(dve.do(V.scalar_tensor_tensor, conv[c:c + 1], out=L.dt[:, c, :], in0=tap,
                                          scalar=conv_w[:, c, j:j + 1], in1=L.dt[:, c, :],
                                          op0=ALU.mult, op1=ALU.add))
                conv = nxt
                yield
            for xs in silu(L.dt, L.tmp, L.xs, conv + [gate]):
                yield
            for c in range(CHUNKS):
                m1 = pe.do(T.matmul, [xs], b0[0:DT_RANK, :], lhsT=W_x[:, c, 0:DT_RANK], rhs=L.xs[:, c, :],
                           start=(c == 0), stop=(c == CHUNKS - 1))
            for c in range(CHUNKS):
                m2 = pe.do(T.matmul, [], b1[0:32, :], lhsT=W_x[:, c, DT_RANK:DT_RANK + 32], rhs=L.xs[:, c, :],
                           start=(c == 0), stop=(c == CHUNKS - 1))
            yield
            dt_r = act.do(A.activation, [m1], L.hT[0:DT_RANK, :], b0[0:DT_RANK, :], ACT.Copy)
            bc = act.do(A.activation, [m2], L.bcs, b1[0:2 * D_STATE, :], ACT.Copy)
            rows_out = sp.dma(L.rows_out, [bc], L.rows_dram, L.bcs)
            yield
            for c, bank in enumerate((b0, b1)):
                m = pe.do(T.matmul, [dt_r, bc], bank, lhsT=W_dt[:, c * P:(c + 1) * P], rhs=L.hT[0:DT_RANK, :],
                          start=True, stop=True)
            dt_mm = m

            def fetch(n, after):
                i = n % 2
                sp.dma(L.rows_in[i], [rows_out] + after, L.Bs[i], L.rows_dram[n].partition_broadcast(P))
                return sp.dma(L.rows_in[i], [], L.Cs[i], L.rows_dram[D_STATE + n].partition_broadcast(P))

            fetched = [fetch(0, []), fetch(1, [dt_mm])]
            Clock.now = dt_mm[2]
            yield
            for c in range(CHUNKS):
                a = act.do(A.activation, [m, xs], L.tmp[:, c, :], L.banks[:, c, :], ACT.Abs, bias=b_dt[:, c:c + 1])
            a = act.do(A.activation, [a], L.tmp, L.tmp, ACT.Exp, scale=-1.0)
            a = act.do(A.activation, [a], L.tmp, L.tmp, ACT.Ln, bias=1.0)
            yield
            for c in range(CHUNKS):
                r = dve.do(V.tensor_scalar, [m, a], out=L.dt[:, c, :], in0=L.banks[:, c, :], scalar1=b_dt[:, c:c + 1],
                           scalar2=0.0, op0=ALU.add, op1=ALU.max)
            dt = dve.do(V.tensor_tensor, [r, a], out=L.dt, in0=L.dt, in1=L.tmp, op=ALU.add)
            z0 = dve.do(V.memset, [dt], L.dA[:, :, 0:1], 0.0)
            dtx = dve.do(V.tensor_tensor, [dt], out=L.dtx, in0=L.dt, in1=L.xs, op=ALU.mult)
            yield
            both = [P, CHUNKS, SEQ]
            flat = lambda ap: ap.rearrange("p c n -> p (c n)")
            scanned, summed = [z0], [rows_out]
            for n in range(D_STATE):
                i = n % 2
                for c in range(CHUNKS):
                    dA = act.do(A.activation, [dt] + scanned, L.dA[:, c, 1:], L.dt[:, c, 1:], ACT.Exp,
                                scale=negA[:, c, n:n + 1])
                m = dve.do(V.tensor_tensor, [fetched[i], dtx] + scanned, out=L.dBx,
                           in0=L.Bs[i].unsqueeze(1).to_broadcast(both), in1=L.dtx, op=ALU.mult)
                yield
                sc = dve.do(V.tensor_tensor_scan, [m, dA] + summed, out=flat(L.h), data0=flat(L.dA),
                            data1=flat(L.dBx), initial=0.0, op0=ALU.mult, op1=ALU.add)
                scanned = [sc]
                yield
                for c in range(CHUNKS):
                    hc = pool.do(G.tensor_tensor, [sc, fetched[i]], out=L.h[:, c, :], in0=L.h[:, c, :],
                                 in1=L.Cs[i], op=ALU.mult)
                    sm = pe.do(T.matmul, [hc, dt], L.banks[:, c, :], lhsT=ident[:], rhs=L.h[:, c, :],
                               start=(n == 0), stop=(n == D_STATE - 1))
                summed = [sm]
                if n + 2 < D_STATE:
                    fetched[i] = fetch(n + 2, [hc, m])
                    Clock.now = sm[2]
                yield
            for c in range(CHUNKS):
                m = dve.do(V.scalar_tensor_tensor, [sm], out=L.xs[:, c, :], in0=L.xs[:, c, :],
                           scalar=skipD[:, c:c + 1], in1=L.banks[:, c, :], op0=ALU.mult, op1=ALU.add)
            m = dve.do(V.tensor_tensor, [m], out=L.xs, in0=L.xs, in1=L.gate, op=ALU.mult)
            yield
            for t in range(TILES):
                for c in range(CHUNKS):
                    p = pe.do(T.matmul, [m], b0[:, t * P:(t + 1) * P], lhsT=L.xs[:, c, t * P:(t + 1) * P],
                              rhs=W_out[:, c, :], start=(c == 0), stop=(c == CHUNKS - 1))
            yield
            m = dve.do(V.tensor_tensor, [p], out=L.x[:], in0=b0.rearrange("p (t n) -> p t n", t=TILES),
                       in1=L.x[:], op=ALU.add)
            L.free = [m]
            yield

        def lane_program(i):
            L = lanes[i]
            stored = []
            for b in range(i, BATCH, LANES):
                if b >= LANES:
                    L.x_here = sp.dma(L.x_in, stored, L.x[:], x_dram[b])
                L.free = [L.x_here] + stored
                yield from macaron_transformer(L)
                yield from alibi_attention(L)
                yield from macaron_transformer(L)
                yield from expert_ffn(L)
                yield from mamba(L)
                yield from expert_ffn(L)
                stored = [sp.dma(L.x_out, L.free, out_dram[b], L.x[:])]
            L.stored = stored

        issue([lane_program(i) for i in range(LANES)], STARTS)
        sp.wait([m for L in lanes for m in L.stored])

        block = ctx.enter_context(nc.Block())

        @block.sync
        def _(eng):
            sp.play(eng)

        @block.tensor
        def _(eng):
            pe.play(eng)

        @block.vector
        def _(eng):
            dve.play(eng)

        @block.scalar
        def _(eng):
            act.play(eng)

        @block.gpsimd
        def _(eng):
            pool.play(eng)



_INS = ["L0_attn_x", "L0_attn_W_qk", "L0_attn_alibi_slope", "L0_ffn_wqkv", "L0_ffn_q_scale", "L0_ffn_k_scale",
        "L0_ffn_wo", "L0_ffn_w1", "L0_ffn_w2", "L0_ffn_b2",
        "L1_attn_W_in", "L1_attn_W_x", "L1_attn_W_dt", "L1_attn_W_out", "L1_ffn_w1", "L1_ffn_w2", "L1_ffn_b2",
        "L1_ffn_gamma", "L1_ffn_beta"]


def kernel(**inputs):
    import concourse.bacc as bacc
    from concourse.bass_utils import run_bass_kernel_spmd

    nc = bacc.Bacc("TRN2", target_bir_lowering=False, num_devices=1)
    arrays = {name: np.ascontiguousarray(inputs[name]) for name in _INS}
    arrays["WvT"] = np.ascontiguousarray(np.asarray(inputs["L0_attn_W_v"]).T)
    arrays["columns"] = parameter_columns(inputs)
    arrays.update(constant_tables())
    d = {n: nc.dram_tensor(f"in_{n}", a.shape, mybir.dt.from_np(a.dtype), kind="ExternalInput").ap()
         for n, a in arrays.items()}
    out = nc.dram_tensor("out_0", (BATCH, SEQ, DIM), F32, kind="ExternalOutput").ap()
    macaron_kernel(nc, d, out)
    r = run_bass_kernel_spmd(nc, [{f"in_{n}": a for n, a in arrays.items()}], core_ids=[0])
    return r.results[0]["out_0"]
```

```python
import numpy as np
import concourse.bass as bass
from concourse import mybir
from contextlib import ExitStack

F32 = mybir.dt.float32
BF16 = mybir.dt.bfloat16
F32R = mybir.dt.float32r
ALU = mybir.AluOpType
ACT = mybir.ActivationFunctionType
AX = mybir.AxisListType

P = 128
BATCH, SEQ, DIM = 8, 512, 128
TILES = SEQ // P
DEPTH, HEADS, HEAD = 2, 8, 64
INNER = HEADS * HEAD
WINDOW = 64
HID = int(DIM * 4 * 2 / 3)
HID_CHUNKS = [(c, min(P, HID - c)) for c in range(0, HID, P)]
PAIRS = INNER // P
QK_SCALE = 8.0
D_INNER, D_STATE, D_CONV, DT_RANK = 256, 16, 4, 64
CHUNKS = D_INNER // P
FF = 512
FF_CHUNKS = FF // P
LN_EPS = 1e-5
MASKED = -1e30
LANES = 4
LEADS = [72000.0, 16000.0, 4000.0, 0.0]
WORK = 6668
BANK = 512


WIDTHS = {"ln": DEPTH * 2, "b1": DEPTH * 2 * 3, "e_b1": FF_CHUNKS, "conv_b": CHUNKS, "b_dt": CHUNKS, "D": CHUNKS,
          "A_log": CHUNKS * D_STATE, "conv_w": CHUNKS * D_CONV}
COLUMNS, COLUMNS_WIDTH = {}, 0
for _name, _width in WIDTHS.items():
    COLUMNS[_name] = (COLUMNS_WIDTH, _width)
    COLUMNS_WIDTH += _width


def parameter_columns(inputs):
    a = {n: np.asarray(inputs[n]) for n in inputs}
    ln = np.stack([a["L0_ffn_ln_g"], a["L0_ffn_ln_b"]], axis=1)
    b1 = a["L0_ffn_b1"].reshape(DEPTH, 2, HID)
    b1 = np.pad(b1, ((0, 0), (0, 0), (0, 3 * P - HID))).reshape(DEPTH, 2, 3, P)

    def by_chunk(v):
        return v.reshape(v.shape[0] // P, P, -1).transpose(1, 0, 2).reshape(P, -1)

    parts = {"ln": ln.transpose(2, 0, 1).reshape(P, -1), "b1": b1.transpose(3, 0, 1, 2).reshape(P, -1),
             "e_b1": by_chunk(a["L1_ffn_b1"][0]), "conv_b": by_chunk(a["L1_attn_conv_b"]),
             "b_dt": by_chunk(a["L1_attn_b_dt"]), "D": by_chunk(a["L1_attn_D"]),
             "A_log": by_chunk(a["L1_attn_A_log"]), "conv_w": by_chunk(a["L1_attn_conv_w"])}
    return np.ascontiguousarray(np.concatenate([parts[n] for n in WIDTHS], axis=1))


def constant_tables():
    f = np.float32
    half = np.arange(0, HEAD, 2, dtype=f)
    inv_freq = f(1.0) / (f(10000.0) ** (half / f(HEAD)))
    t = np.arange(SEQ, dtype=f)
    freqs = t[:, None] * inv_freq[None, :]
    freqs = np.concatenate([freqs, freqs], axis=-1)
    base = (half + f(0.4 * HEAD)) / f(1.4 * HEAD)
    power = (t - SEQ // 2) / f(WINDOW // 2)
    scale = base[None, :] ** power[:, None]
    scale = np.concatenate([scale, scale], axis=-1).astype(f)
    cos, sin = np.cos(freqs).astype(f), np.sin(freqs).astype(f)
    sign = np.concatenate([-np.ones(HEAD // 2, f), np.ones(HEAD // 2, f)])
    rotary = np.stack([cos * scale, cos / scale, sin * scale * sign, sin / scale * sign])
    rotary = rotary.reshape(2, 2, TILES, P, HEAD).transpose(3, 0, 2, 1, 4)

    row, col = np.arange(P)[:, None], np.arange(P)[None, :]
    even = row < WINDOW
    key = np.where(even & (col >= WINDOW), col - P, col)
    seen = (key <= row) & (row <= key + WINDOW)
    first = seen & (key >= 0)
    local = np.stack([np.where(m, 0.0, MASKED) for m in (first, seen)])
    local = local.transpose(1, 0, 2)

    rel = (np.arange(SEQ)[None, :] - (SEQ - P) - row).astype(f)
    causal = np.where(rel <= 0, 0.0, MASKED).astype(f)

    shift = np.stack([np.eye(P, k=1, dtype=f), np.eye(P, k=1 - P, dtype=f)]).transpose(1, 0, 2)

    bf = mybir.dt.np(BF16)
    return {
        "c_rotary": np.ascontiguousarray(rotary, f),
        "c_local": np.ascontiguousarray(local.astype(bf)),
        "c_rel": rel,
        "c_causal": causal,
        "c_ident": np.eye(P, dtype=f),
        "c_shift": np.ascontiguousarray(shift),
        "c_ident16": np.eye(P, dtype=f).astype(bf),
    }


TABLES = {ACT.Exp: "exp", ACT.Tanh: "exp", ACT.Gelu: "gelu", ACT.Ln: "ln"}


class Instruction:

    def __init__(self, engine, method, after, args, kw, counter=None):
        self.engine, self.method, self.after, self.args, self.kw = engine, method, after, args, kw
        self.counter, self.place, self.ends = counter, None, None
        if counter is not None:
            counter.value += 16
            self.place = (counter.sem, counter.value)


class Engine:

    def __init__(self, sem, fixed, per_element, latency, notice):
        self.sem, self.count, self.items, self.seen = sem, 0, [], {}
        self.fixed, self.per_element, self.free_at = fixed, per_element, 0.0
        self.latency, self.notice = latency, notice
        self.state = None
        self.recorded = []

    def do(self, method, after, *args, **kw):
        instruction = Instruction(self, method, after, args, kw)
        self.recorded.append(instruction)
        return instruction

    def dma(self, counter, after, out, in_):
        instruction = Instruction(self, self.dma_method, after, (out, in_), {}, counter)
        self.recorded.append(instruction)
        return instruction

    def taken(self):
        instructions, self.recorded = self.recorded, []
        return instructions

    def wait(self, after):
        for i in after:
            sem, value = i.place
            if self.seen.get(id(sem), 0) < value:
                self.seen[id(sem)] = value
                self.items.append((sem, value))

    def start(self, i):
        return max([self.free_at] + [a.ends + self.notice for a in i.after])

    def queue(self, i):
        time = self.cost(i)
        self.free_at = self.start(i) + self.switch(i) + time
        if self.needs(i):
            self.state = self.needs(i)
        self.wait(i.after)
        self.items.append(i)
        if i.counter is None:
            self.count += 1
            i.place = (self.sem, self.count)
        i.ends = self.free_at + self.lag(i)
        return time

    def lag(self, i):
        large = i.counter is not None and i.args[0].partition_size() * i.args[0].free_size() > P * P
        return self.latency + 1000.0 * large

    def needs(self, i):
        if "rhs" in i.kw or "identity" in i.kw:
            still = i.kw["lhsT"] if "lhsT" in i.kw else i.args[1]
            return (still.partition_size() > HEAD, still.free_size() > HEAD)
        return TABLES.get(i.args[2]) if len(i.args) > 2 and isinstance(i.args[2], ACT) else None

    def switch(self, i):
        if self.needs(i) in (None, self.state):
            return 0.0
        return 64.0 if "rhs" in i.kw or "identity" in i.kw else 1283.0

    def cost(self, i):
        args, kw = i.args, i.kw
        extra = 0.0
        if i.counter is not None:
            elements = 0
        elif "rhs" in kw or "identity" in kw:
            moving = kw["rhs"] if "rhs" in kw else kw["identity"]
            passes = 1 if moving.dtype in (BF16, F32R) else 2 if "rhs" not in kw or kw.get("is_transpose") else 4
            elements = moving.free_size() * passes
            if not self.needs(i)[1]:
                extra, elements = 26.0, elements / 2
        else:
            elements = max(a.free_size() for a in list(args) + list(kw.values()) if isinstance(a, bass.AP))
            if kw.get("op") == ALU.pow:
                extra = 188.0 * elements
            if isinstance(kw.get("scalar"), bass.AP) or isinstance(kw.get("scalar1"), bass.AP):
                extra = 50.0
            extra += 93.0 * sum(isinstance(kw.get(n), bass.AP) for n in ("bias", "scale"))
            if len(args) > 2 and isinstance(args[2], ACT) and args[1].space != bass.MemoryType.PSUM:
                extra += 44.0
        return extra + self.fixed + self.per_element * elements

    def play(self, eng):
        for item in self.items:
            if isinstance(item, tuple):
                eng.wait_ge(*item)
            elif item.counter is not None:
                item.method(*item.args, **item.kw).then_inc(item.counter.sem, 16)
            else:
                item.method(*item.args, **item.kw).then_inc(self.sem, 1)


class DmaCount:

    def __init__(self, sem):
        self.sem, self.value = sem, 0


def fill_queues(engines, programs):
    heads = [[0] * len(engines) for _ in programs]
    used = [-lead for lead in LEADS]
    left = sum(len(queue) for program in programs for queue in program)
    while left:
        best = None
        for n, program in enumerate(programs):
            for e, engine in enumerate(engines):
                if heads[n][e] < len(program[e]):
                    i = program[e][heads[n][e]]
                    if all(a.ends is not None for a in i.after):
                        key = (engine.start(i) + engine.switch(i), used[n])
                        if best is None or key < best[0]:
                            best = (key, n, e)
        _, n, e = best
        queue = programs[n][e]
        while True:
            used[n] += engines[e].queue(queue[heads[n][e]])
            heads[n][e] += 1
            left -= 1
            if heads[n][e] == len(queue) or queue[heads[n][e]].after:
                break


def macaron_kernel(nc, d, out_d):
    ctx = ExitStack()
    with ctx:
        def sb(name, shape, dt=F32):
            return ctx.enter_context(nc.sbuf_tensor(name, shape, dt))

        def sem(name):
            return ctx.enter_context(nc.semaphore(name))

        pe = Engine(sem("pe_done"), 0.0, 0.42, 200.0, 75.0)
        dve = Engine(sem("dve_done"), 68.0, 1.04, 127.0, 0.0)
        act = Engine(sem("act_done"), 52.0, 0.83, 150.0, 0.0)
        pool = Engine(sem("pool_done"), 110.0, 2.2, 65.0, 30.0)
        sp = Engine(sem("sp_done"), 60.0, 0.0, 2200.0, 0.0)
        engines = [pe, dve, act, pool, sp]
        sp.dma_method = nc.sync.dma_start
        V, A, G, T = nc.vector, nc.scalar, nc.gpsimd, nc.tensor

        ident = sb("ident", [P, P])
        ident16 = sb("ident16", [P, P], BF16)
        shift = sb("shift", [P, 2, P])
        local_mask = sb("local_mask", [P, 2, P], BF16)
        alibi = sb("alibi", [P, SEQ])
        slope = sb("slope", [P, 1])
        rot = [sb(f"rot{l}", [P, 2, TILES, 2, HEAD]) for l in range(DEPTH)]
        wqkv_hi = sb("wqkv_hi", [P, DEPTH, 3 * INNER], F32R)
        wqkv_lo = sb("wqkv_lo", [P, DEPTH, 3 * INNER], F32R)
        wo = sb("wo", [P, DEPTH, PAIRS, DIM])
        columns = sb("columns", [P, COLUMNS_WIDTH])
        col = {n: columns[:, at:at + w] for n, (at, w) in COLUMNS.items()}
        lnT = col["ln"].rearrange("p (l a) -> p l a", l=DEPTH)
        w1 = sb("w1", [P, DEPTH, 2 * HID])
        b1T = col["b1"].rearrange("p (l a c) -> p l a c", l=DEPTH, a=2)
        w2 = sb("w2", [P, DEPTH, 3, DIM])
        Wqk = sb("Wqk", [P, DIM])
        WvT = sb("WvT", [P, DIM])
        W_in = sb("W_in", [P, 2 * D_INNER])
        conv_w = col["conv_w"].rearrange("p (c j) -> p c j", c=CHUNKS)
        conv_b = col["conv_b"]
        W_x = sb("W_x", [P, CHUNKS, DT_RANK + 2 * D_STATE])
        W_dt = sb("W_dt", [DT_RANK, D_INNER])
        b_dt = col["b_dt"]
        negA = sb("negA", [P, CHUNKS, D_STATE])
        skipD = col["D"]
        W_out = sb("W_out", [P, CHUNKS, DIM])
        e_w1 = sb("e_w1", [P, FF])
        e_b1 = col["e_b1"]
        e_w2 = sb("e_w2", [P, FF_CHUNKS, DIM])
        e_b2 = sb("e_b2", [P, DIM])
        gamma = sb("gamma", [P, DIM])
        beta = sb("beta", [P, DIM])
        neg_half = sb("neg_half", [P, 16])

        loaded = DmaCount(sem("weights_loaded"))

        def load(dst, src):
            return sp.dma(loaded, [], dst, src)

        class Lane:
            pass

        def new_lane(i):
            L = Lane()
            L.x = sb(f"x{i}", [P, TILES, DIM])
            spare = sb(f"spare{i}", [P, 2, TILES, DIM])
            L.y, L.xn = spare[:, 0], spare[:, 1]
            L.hT = sb(f"hT{i}", [P, SEQ])
            L.hT_hi = sb(f"hT_hi{i}", [P, P], F32R)
            L.hT_lo = sb(f"hT_lo{i}", [P, P], F32R)
            L.stats = sb(f"stats{i}", [P, TILES, 6])
            L.mv = sb(f"mv{i}", [P, TILES, 2])
            L.rstd = sb(f"rstd{i}", [P, TILES])
            L.ss = sb(f"ss{i}", [P, 16])
            L.rn = sb(f"rn{i}", [P, 16])
            L.mx = sb(f"mx{i}", [P, HEADS])
            L.rs = sb(f"rs{i}", [P, HEADS])
            L.work = sb(f"work{i}", [P, WORK])
            L.banks = ctx.enter_context(nc.psum_tensor(f"banks{i}", [P, 2, BANK], F32))
            L.x_in = DmaCount(sem(f"x_in{i}"))
            L.x_out = DmaCount(sem(f"x_out{i}"))
            L.v_in = DmaCount(sem(f"v_in{i}"))
            L.rows_out = DmaCount(sem(f"rows_out{i}"))
            L.rows_in = [DmaCount(sem(f"rows_in{i}_{k}")) for k in range(2)]
            L.rows_dram = nc.dram_tensor(f"bc_rows{i}", (2 * D_STATE, SEQ), F32, kind="Internal").ap()

            at = [0]

            def cut(*shape):
                n = int(np.prod(shape))
                ap = L.work[:, at[0]:at[0] + n]
                at[0] += n
                assert at[0] <= WORK
                if len(shape) == 2:
                    ap = ap.rearrange("p (a b) -> p a b", a=shape[0])
                elif len(shape) == 3:
                    ap = ap.rearrange("p (a b c) -> p a b c", a=shape[0], b=shape[1])
                return ap

            L.sq = L.ts = cut(16, HEAD)
            L.tq = cut(16, HEAD)
            L.tc = cut(16, HEAD)
            L.prob = L.tq.rearrange("p (a b) d -> p a (b d)", b=2)
            L.probT = L.tc.rearrange("p (a b) d -> p a (b d)", b=2)
            L.o, L.oT = L.prob[:, 0:4, :], L.probT[:, 0:4, :]
            L.qT = cut(PAIRS, P)
            L.kT = cut(2, PAIRS, P)
            L.V = [cut(HEADS, HEAD + 1) for _ in range(2)]
            L.Vc = cut(HEADS, HEAD + 1)
            at[0] = 0
            L.hid = cut(3, SEQ)
            L.gelu = [cut(SEQ) for _ in range(2)]
            at[0] = 0
            L.uT = cut(SEQ)
            L.va = cut(TILES, DIM)
            L.ap = cut(SEQ)
            L.apT = cut(TILES, P)
            at[0] = 0
            L.gate = spare[:].rearrange("p c t n -> p c (t n)")
            L.xc = cut(CHUNKS, SEQ + D_CONV - 1)
            L.dBx = L.work[:, 0:CHUNKS * SEQ].rearrange("p (c n) -> p c n", c=CHUNKS)
            L.xs = L.dtx = L.gated = cut(CHUNKS, SEQ)
            L.dt = cut(CHUNKS, SEQ)
            L.dA = L.tmp = cut(CHUNKS, SEQ)
            L.h = cut(CHUNKS, SEQ)
            L.bcs = L.h.rearrange("p c n -> p (c n)")[0:2 * D_STATE, 0:SEQ]
            L.Bs = [cut(SEQ) for _ in range(2)]
            L.Cs = [cut(SEQ), L.hT[:]]
            at[0] = 0
            L.eh = cut(FF_CHUNKS, SEQ)
            L.r = L.y
            return L

        lanes = [new_lane(i) for i in range(LANES)]
        rot_base = lanes[-1].work[:, 0:1024].rearrange("p (a t b d) -> p a t b d", a=2, t=TILES, b=2)
        rel = lanes[-1].work[:, 1024:1024 + SEQ]
        qk_gain = lanes[-1].work[:, 1536:1536 + DEPTH * 2 * HEAD].rearrange("p (l b d) -> p l b d", l=DEPTH, b=2)
        wqkv = lanes[-1].work[:, 2048:2048 + DEPTH * 3 * INNER].rearrange("p (l n) -> p l n", l=DEPTH)
        x_dram = d["L0_attn_x"].rearrange("b (t p) d -> b p t d", p=P)
        out_dram = out_d.rearrange("b (t p) d -> b p t d", p=P)

        for i, L in enumerate(lanes):
            L.x_here = sp.dma(L.x_in, [], L.x[:], x_dram[i])
        load(ident[:], d["c_ident"])
        load(ident16[:], d["c_ident16"])
        load(shift[:], d["c_shift"])
        load(wqkv, d["L0_ffn_wqkv"].rearrange("l k n -> k l n"))
        load(rot_base, d["c_rotary"])
        for l in range(DEPTH):
            load(qk_gain[:, l, 0, :], d["L0_ffn_q_scale"][l].partition_broadcast(P))
            load(qk_gain[:, l, 1, :], d["L0_ffn_k_scale"][l].partition_broadcast(P))
        load(local_mask[:], d["c_local"])
        for l in range(DEPTH):
            rows = d["L0_ffn_wo"][l].rearrange("(c j b d) n -> j d b c n", c=2, j=2, b=2)
            for j in range(2):
                for b in range(2):
                    load(wo[j * HEAD:(j + 1) * HEAD, l, 2 * b:2 * b + 2, :], rows[j, :, b])
        load(w1[:], d["L0_ffn_w1"].rearrange("l k n -> k l n"))
        for c, (c0, n) in enumerate(HID_CHUNKS):
            for l in range(DEPTH):
                load(w2[0:n, l, c, :], d["L0_ffn_w2"][l, c0:c0 + n, :])
        last_rows = HID_CHUNKS[-1][1]
        for l in range(DEPTH):
            load(w2[last_rows:last_rows + 1, l, 2, :], d["L0_ffn_b2"][l:l + 1, :])
        load(columns[:], d["columns"])
        load(Wqk[:], d["L0_attn_W_qk"])
        load(WvT[:], d["WvT"])
        load(slope[:], d["L0_attn_alibi_slope"].partition_broadcast(P))
        load(rel, d["c_rel"])
        load(alibi[:], d["c_causal"])
        load(e_w1[:], d["L1_ffn_w1"][0])
        load(e_w2[:], d["L1_ffn_w2"][0].rearrange("(c p) n -> p c n", p=P))
        load(e_b2[:], d["L1_ffn_b2"][0].partition_broadcast(P))
        load(gamma[:], d["L1_ffn_gamma"].partition_broadcast(P))
        load(beta[:], d["L1_ffn_beta"].partition_broadcast(P))
        load(W_in[:], d["L1_attn_W_in"])
        load(W_x[:], d["L1_attn_W_x"].rearrange("(c p) n -> p c n", p=P))
        load(W_dt[:], d["L1_attn_W_dt"])
        weights = load(W_out[:], d["L1_attn_W_out"].rearrange("(c p) n -> p c n", p=P))

        H2 = HEAD // 2
        const = pool.do(G.memset, [], neg_half[:], -0.5)
        high = dve.do(V.tensor_copy, [weights], wqkv_hi[:], wqkv)
        dve.do(V.tensor_tensor, [high], out=wqkv_lo[:], in0=wqkv, in1=wqkv_hi[:].bitcast(F32), op=ALU.subtract)
        for l in range(DEPTH):
            g = qk_gain[:, l].unsqueeze(1)
            full = [P, TILES, 2, HEAD]
            half = [P, TILES, 2, H2]
            dve.do(V.tensor_tensor, [weights], out=rot[l][:, 0], in0=rot_base[:, 0],
                   in1=g.to_broadcast(full), op=ALU.mult)
            dve.do(V.tensor_tensor, [], out=rot[l][:, 1, :, :, 0:H2], in0=rot_base[:, 1, :, :, 0:H2],
                   in1=g[:, :, :, H2:HEAD].to_broadcast(half), op=ALU.mult)
            dve.do(V.tensor_tensor, [], out=rot[l][:, 1, :, :, H2:HEAD], in0=rot_base[:, 1, :, :, H2:HEAD],
                   in1=g[:, :, :, 0:H2].to_broadcast(half), op=ALU.mult)
        dve.do(V.scalar_tensor_tensor, [], out=alibi[:], in0=rel, scalar=slope[:, 0:1],
               in1=alibi[:], op0=ALU.mult, op1=ALU.add)
        A_log = col["A_log"].rearrange("p (c n) -> p c n", c=CHUNKS)
        exp_A = act.do(A.activation, [weights], negA[:], A_log, ACT.Exp)
        tables = dve.do(V.tensor_scalar, [exp_A], out=negA[:], in0=negA[:], scalar1=-1.0, scalar2=None,
                        op0=ALU.mult)
        ready = [weights, tables, const]


        def layer_norm(L, src, dst, after):
            for t in range(TILES):
                m = dve.do(V.bn_stats, after, L.stats[:, t, :], src[:, t, :])
            for t in range(TILES):
                m = dve.do(V.bn_aggr, [m], L.mv[:, t, :], L.stats[:, t, :])
            m = dve.do(V.tensor_scalar, [m], out=L.rstd[:], in0=L.mv[:, :, 1], scalar1=LN_EPS, scalar2=None,
                       op0=ALU.add)
            m = pool.do(G.tensor_tensor, [m, const], out=L.rstd[:], in0=L.rstd[:], in1=neg_half[:, 0:TILES],
                        op=ALU.pow)
            for t in range(TILES):
                m = dve.do(V.tensor_scalar, [m], out=dst[:, t, :], in0=src[:, t, :],
                           scalar1=L.mv[:, t, 0:1], scalar2=L.rstd[:, t:t + 1],
                           op0=ALU.subtract, op1=ALU.mult)
            L.normed = m

        def to_features(L, src, bank, after):
            for t in range(TILES):
                m = pe.do(T.transpose, after, bank[:, t * P:(t + 1) * P], src[:, t, :], identity=ident[:])
            return m

        def project(L, l, t):
            hT = L.hT[:, t * P:(t + 1) * P]
            b0, b1 = banks = [L.banks[:, 0, :], L.banks[:, 1, :]]
            heads = [b.rearrange("p (h d) -> p h d", d=HEAD) for b in banks]
            half = [slice(0, HEADS), slice(HEADS, 2 * HEADS)]
            high = act.do(A.activation, L.hT_here + L.parts_read, L.hT_hi[:], hT, ACT.Copy)
            parts = dve.do(V.tensor_tensor, [high] + L.parts_read, out=L.hT_lo[:], in0=hT,
                           in1=L.hT_hi[:].bitcast(F32), op=ALU.subtract)

            def product(bank, s, after):
                w = [x[:, l, s * INNER:(s + 1) * INNER] for x in (wqkv_hi, wqkv_lo)]
                pe.do(T.matmul, [parts] + after, bank, lhsT=L.hT_hi[:], rhs=w[0], start=True, stop=False)
                pe.do(T.matmul, [], bank, lhsT=L.hT_hi[:], rhs=w[1], start=False, stop=False)
                return pe.do(T.matmul, [], bank, lhsT=L.hT_lo[:], rhs=w[0], start=False, stop=True)

            made = [product(banks[s], s, L.free) for s in range(2)]
            squared = [act.do(A.activation, [made[s]] + L.free, L.sq[:, half[s]], heads[s], ACT.Square)
                       for s in range(2)]
            norm = []
            for s in range(2):
                ss, rn = L.ss[:, half[s]], L.rn[:, half[s]]
                m = dve.do(V.tensor_reduce, [squared[s]], out=ss, in_=L.sq[:, half[s]], axis=AX.X, op=ALU.add)
                m = pool.do(G.tensor_scalar, [m], out=ss, in0=ss, scalar1=1e-24, scalar2=None, op0=ALU.max)
                norm.append(pool.do(G.tensor_tensor, [m, const], out=rn, in0=ss, in1=neg_half[:, half[s]], op=ALU.pow))
            sined, cosined, unit = [], [], []
            for s in range(2):
                unit.append(dve.do(V.tensor_tensor, [norm[s], made[s]], out=L.tq[:, half[s]], in0=heads[s],
                                   in1=L.rn[:, half[s]].unsqueeze(2).to_broadcast([P, HEADS, HEAD]), op=ALU.mult))
                if s == 0:
                    v = product(b0, 2, [unit[0]])
                    L.parts_read = [v]
                cosined.append(pool.do(G.tensor_tensor, [unit[s]], out=L.tc[:, half[s]], in0=L.tq[:, half[s]],
                                       in1=rot[l][:, 0, t, s].unsqueeze(1).to_broadcast([P, HEADS, HEAD]),
                                       op=ALU.mult))
            for s in range(2):
                split = [P, HEADS, 2, H2]
                sined.append(dve.do(V.tensor_tensor, [unit[s]],
                                    out=L.ts[:, half[s]].rearrange("p h (a d) -> p h a d", a=2),
                                    in0=L.tq[:, half[s]].rearrange("p h (a d) -> p h a d", a=2)[:, :, ::-1, :],
                                    in1=rot[l][:, 1, t, s].rearrange("p (a d) -> p a d", a=2).unsqueeze(1)
                                    .to_broadcast(split), op=ALU.mult))
            v_copied = act.do(A.activation, [v], L.V[t % 2][:, :, 0:HEAD], heads[0], ACT.Copy)
            v_dma = sp.dma(L.v_in, [v_copied], L.Vc[0:WINDOW], L.V[t % 2][0:WINDOW])
            if t > 0:
                v_dma = sp.dma(L.v_in, [], L.Vc[WINDOW:P], L.V[(t - 1) % 2][WINDOW:P])
            tcf = L.tc.rearrange("p (c h) d -> p c (h d)", h=2)
            turned = []
            for s, bank in ((0, b1), (1, b0)):
                tc, ts = L.tc[:, half[s]], L.ts[:, half[s]]
                whole = pool.do(G.tensor_tensor, [cosined[s], sined[s]], out=tc, in0=tc, in1=ts, op=ALU.add)
                for c in range(PAIRS):
                    m = pe.do(T.transpose, [whole, v_copied, unit[1]] if c == 0 else [], bank[:, c * P:(c + 1) * P],
                              tcf[:, s * PAIRS + c, :], identity=ident[:])
                turned.append(m)
            q_copied = act.do(A.activation, [turned[0]], L.qT, b1.rearrange("p (c n) -> p c n", c=PAIRS), ACT.Copy)
            k_copied = act.do(A.activation, [turned[1]], L.kT[:, t % 2], b0.rearrange("p (c n) -> p c n", c=PAIRS),
                              ACT.Copy)
            L.qk_here = [q_copied, k_copied]
            L.v_here = [v_copied, v_dma]

        def local_attention(L, l, t):
            mask = local_mask[:, min(t, 1), :].unsqueeze(1).to_broadcast([P, 4, P])
            W1 = HEAD + 1
            banks = [L.banks[:, b, :] for b in range(2)]
            s4 = [b.rearrange("p (j n) -> p j n", n=P) for b in banks]
            prob = [L.prob[:, 4 * b:4 * b + 4, :] for b in range(2)]
            probT = [L.probT[:, 4 * b:4 * b + 4, :] for b in range(2)]
            for b in range(2):
                pe.do(T.matmul, L.qk_here, s4[b], lhsT=ident16[:], rhs=mask, start=True, stop=False,
                      skip_group_check=True)

            blocks = L.kT.rearrange("p s c n -> p (s c n)").rearrange("p (k n) -> p k n", n=WINDOW)
            half = 2 * PAIRS
            scored = []
            for b in range(2):
                rows = slice(b * HEAD, (b + 1) * HEAD)
                for j in range(4):
                    own = (t % 2) * half + 2 * j
                    if t == 0:
                        even = blocks[rows, own:own + 2, :]
                    elif t % 2 == 0:
                        even = blocks[rows, own:own + half + 2:half + 1, :]
                    else:
                        even = blocks[rows, own:own - half:1 - half, :]
                    pe.do(T.matmul, [], s4[b][0:WINDOW, j, :], lhsT=L.qT[rows, j, 0:WINDOW], rhs=even,
                          start=False, stop=True, skip_group_check=True)
                    m = pe.do(T.matmul, [], s4[b][WINDOW:P, j, :], lhsT=L.qT[rows, j, WINDOW:P],
                              rhs=L.kT[rows, t % 2, j, :], start=False, stop=True, skip_group_check=True)
                scored.append(m)
            top, lowered, raised, turned, copied = [], [], [], [], []
            for b in range(2):
                top.append(dve.do(V.tensor_reduce, [scored[b]], out=L.mx[:, 4 * b:4 * b + 4], in_=s4[b],
                                  axis=AX.X, op=ALU.max, negate=True))
            for b in range(2):
                lowered.append(dve.do(V.tensor_tensor, [top[b]], out=prob[b], in0=s4[b],
                                      in1=L.mx[:, 4 * b:4 * b + 4].unsqueeze(2).to_broadcast([P, 4, P]),
                                      op=ALU.add))
                raised.append(act.do(A.activation, [lowered[b]], prob[b], prob[b], ACT.Exp, scale=QK_SCALE))
            for b in range(2):
                for j in range(4):
                    m = pe.do(T.transpose, [raised[b]], banks[b][:, j * P:(j + 1) * P], prob[b][:, j, :],
                              identity=ident[:])
                turned.append(m)
            for b in range(2):
                copied.append(act.do(A.activation, [turned[b]], probT[b], s4[b], ACT.Copy))
            weighted, divided = [], []
            for b in range(2):
                for j in range(4):
                    h = 2 * j + b
                    dst = banks[b][:, j * W1:(j + 1) * W1]
                    pe.do(T.matmul, [copied[b]] + L.v_here, dst[0:WINDOW], lhsT=probT[b][:, j, 0:WINDOW],
                             rhs=L.Vc[:, h, :], start=True, stop=True)
                    m = pe.do(T.matmul, [], dst[WINDOW:P], lhsT=probT[b][:, j, WINDOW:P],
                              rhs=L.V[t % 2][:, h, :], start=True, stop=True)
                weighted.append(m)
            inverse = []
            o = [b[:, 0:4 * W1].rearrange("p (j w) -> p j w", w=W1) for b in banks]
            for b in range(2):
                inverse.append(dve.do(V.reciprocal, [weighted[b]], L.rs[:, 4 * b:4 * b + 4], o[b][:, :, HEAD]))
            for b in range(2):
                divided.append(dve.do(V.tensor_tensor, [inverse[b]],
                                      out=L.o[:, 2 * b:2 * b + 2, :].rearrange("p c (a d) -> p (c a) d", a=2),
                                      in0=o[b][:, :, 0:HEAD],
                                      in1=L.rs[:, 4 * b:4 * b + 4].unsqueeze(2).to_broadcast([P, 4, HEAD]),
                                      op=ALU.mult))
            o_turned, oT = [], []
            for b in range(2):
                for c in range(2):
                    m = pe.do(T.transpose, [divided[b]], banks[b][:, c * P:(c + 1) * P], L.o[:, 2 * b + c, :],
                              identity=ident[:])
                o_turned.append(m)
            for b in range(2):
                oT.append(act.do(A.activation, [o_turned[b]], L.oT[:, 2 * b:2 * b + 2, :],
                                 banks[b][:, 0:2 * P].rearrange("p (c n) -> p c n", c=2), ACT.Copy))
            for c in range(PAIRS):
                m = pe.do(T.matmul, [oT[c // 2]], banks[0][:, 0:DIM], lhsT=L.oT[:, c, :], rhs=wo[:, l, c, :],
                          start=(c == 0), stop=(c == PAIRS - 1))
            added = dve.do(V.tensor_tensor, [m], out=L.y[:, t, :], in0=banks[0][:, 0:DIM], in1=L.y[:, t, :],
                           op=ALU.add)
            L.free = [added, oT[1]]

        def transformer_layer(L, l):
            b0, b1 = L.banks[:, 0, :], L.banks[:, 1, :]
            m = to_features(L, L.y, b0, L.free)
            a = act.do(A.activation, [m], L.hT[0:HEAD, :], b0[0:HEAD, :], ACT.Copy)
            b = act.do(A.activation, [], L.hT[HEAD:P, 1:SEQ], b0[HEAD:P, 0:SEQ - 1], ACT.Copy)
            z = dve.do(V.memset, L.free, L.hT[HEAD:P, 0:1], 0.0)
            zv = pool.do(G.memset, L.free, L.Vc, 0.0)
            L.free = [a, b, z, zv]
            L.hT_here, L.parts_read = [b, z], [b]
            for t in range(TILES):
                project(L, l, t)
                local_attention(L, l, t)
            first = pool.do(G.tensor_copy, L.free, L.xn[:, :, 0:HEAD], L.y[:, :, 0:HEAD])
            moved = b1[:, 0:TILES * HEAD].rearrange("p (t n) -> p t n", t=TILES)
            pe.do(T.matmul, L.free, moved, lhsT=shift[:, 0, :], rhs=L.y[:, :, HEAD:DIM], start=True, stop=False,
                  skip_group_check=True)
            m = pe.do(T.matmul, [], moved[:, 1:TILES, :], lhsT=shift[:, 1, :], rhs=L.y[:, 0:TILES - 1, HEAD:DIM],
                      start=False, stop=True, skip_group_check=True)
            second = act.do(A.activation, [m] + L.free, L.xn[:, :, HEAD:DIM], moved, ACT.Copy)
            layer_norm(L, L.xn, L.xn, [first, second])
            m = to_features(L, L.xn, b0, [L.normed])
            hT = act.do(A.activation, [m], L.hT[:], b0, ACT.Identity, bias=lnT[:, l, 1:2], scale=lnT[:, l, 0:1])
            ones = dve.do(V.memset, L.free, L.hid[HEAD:P, 2, :], 1.0)
            g_free, u_free = [], []
            for c, (c0, n) in enumerate(HID_CHUNKS):
                g = pe.do(T.matmul, [hT] + g_free, b1[0:n, :], lhsT=w1[:, l, HID + c0:HID + c0 + n], rhs=L.hT[:],
                          start=True, stop=True)
                u = pe.do(T.matmul, u_free, b0[0:n, :], lhsT=w1[:, l, c0:c0 + n], rhs=L.hT[:], start=True, stop=True)
                gelu_old = u_free if c == 2 else []
                g_free = [act.do(A.activation, [g] + gelu_old, L.gelu[c % 2][0:n, :], b1[0:n, :], ACT.Gelu,
                                 bias=b1T[0:n, l, 1, c:c + 1])]
                hd = dve.do(V.scalar_tensor_tensor, [u, g_free[0], ones], out=L.hid[0:n, c, :], in0=b0[0:n, :],
                            scalar=b1T[0:n, l, 0, c:c + 1], in1=L.gelu[c % 2][0:n, :],
                            op0=ALU.add, op1=ALU.mult)
                u_free = [hd]
            for t in range(TILES):
                for c, (c0, n) in enumerate(HID_CHUNKS):
                    k = n + 1 if c == 2 else n
                    m = pe.do(T.matmul, [hd], b1[:, t * P:(t + 1) * P], lhsT=L.hid[0:k, c, t * P:(t + 1) * P],
                              rhs=w2[0:k, l, c, :], start=(c == 0), stop=(c == 2))
            m = dve.do(V.tensor_tensor, [m], out=L.y, in0=b1.rearrange("p (t n) -> p t n", t=TILES),
                       in1=L.y, op=ALU.add)
            L.free = [m]

        def macaron_transformer(L):
            for v in L.V:
                ones = pool.do(G.memset, L.free + ready, v[:, :, HEAD:HEAD + 1], 1.0)
            layer_norm(L, L.x[:], L.y, L.free)
            L.free = [L.normed, ones]
            for l in range(DEPTH):
                if l:
                    for v in L.V:
                        ones = pool.do(G.memset, L.free, v[:, :, HEAD:HEAD + 1], 1.0)
                    L.free = L.free + [ones]
                transformer_layer(L, l)
            m = dve.do(V.scalar_tensor_tensor, L.free, out=L.x[:], in0=L.y, scalar=0.5, in1=L.x[:],
                       op0=ALU.mult, op1=ALU.add)
            L.free = [m]

        def alibi_attention(L):
            b0, b1 = L.banks[:, 0, :], L.banks[:, 1, :]
            layer_norm(L, L.x[:], L.xn, L.free)
            m = to_features(L, L.xn, b0, [L.normed])
            xT = act.do(A.activation, [m], L.hT[:], b0, ACT.Copy)
            m = pe.do(T.matmul, [xT], b1, lhsT=Wqk[:], rhs=L.hT[:], start=True, stop=True)
            uT = act.do(A.activation, [m], L.uT, b1, ACT.Copy)
            for t in range(TILES):
                m = pe.do(T.matmul, [], b0[:, t * P:(t + 1) * P], lhsT=L.hT[:, t * P:(t + 1) * P], rhs=WvT[:],
                          start=True, stop=True)
            va = act.do(A.activation, [m], L.va, b0.rearrange("p (t n) -> p t n", t=TILES), ACT.Copy)
            scale = float(np.float32(1.0 / np.sqrt(DIM)))
            free = [va]
            for t in range(TILES):
                n = (t + 1) * P
                m = pe.do(T.matmul, [uT] + free, b0[:, 0:n], lhsT=L.uT[:, t * P:(t + 1) * P],
                          rhs=L.hT[:, 0:n], start=True, stop=True)
                sc = dve.do(V.scalar_tensor_tensor, [m], out=L.ap[:, 0:n], in0=b0[:, 0:n], scalar=scale,
                            in1=alibi[:, SEQ - n:SEQ], op0=ALU.mult, op1=ALU.add)
                m = dve.do(V.tensor_reduce, [sc], out=L.mx[:, 0:1], in_=L.ap[:, 0:n], axis=AX.X, op=ALU.max,
                           negate=True)
                ex = act.do(A.activation, [m], L.ap[:, 0:n], L.ap[:, 0:n], ACT.Exp,
                            bias=L.mx[:, 0:1], accum_out=L.rs[:, 0:1])
                for k in range(t + 1):
                    m = pe.do(T.transpose, [ex], b1[:, k * P:(k + 1) * P], L.ap[:, k * P:(k + 1) * P],
                              identity=ident[:])
                r = dve.do(V.reciprocal, [ex], L.rs[:, 1:2], L.rs[:, 0:1])
                pT = act.do(A.activation, [m], L.apT[:, 0:t + 1, :],
                            b1[:, 0:n].rearrange("p (t n) -> p t n", t=t + 1), ACT.Copy)
                for k in range(t + 1):
                    m = pe.do(T.matmul, [pT], b0[:, 0:DIM], lhsT=L.apT[:, k, :], rhs=L.va[:, k, :],
                              start=(k == 0), stop=(k == t))
                xd = dve.do(V.scalar_tensor_tensor, [m, r], out=L.x[:, t, :], in0=b0[:, 0:DIM],
                            scalar=L.rs[:, 1:2], in1=L.x[:, t, :], op0=ALU.mult, op1=ALU.add)
                free = [xd]
            L.free = [xd]

        def expert_ffn(L):
            banks = [L.banks[:, 1, :], L.banks[:, 0, :]]
            layer_norm(L, L.x[:], L.xn, L.free)
            m = to_features(L, L.xn, banks[1], [L.normed])
            xT = act.do(A.activation, [m], L.hT[:], banks[1], ACT.Copy)
            done = [[], [xT]]
            for c in range(FF_CHUNKS):
                m = pe.do(T.matmul, [xT] + done[c % 2], banks[c % 2], lhsT=e_w1[:, c * P:(c + 1) * P],
                          rhs=L.hT[:], start=True, stop=True)
                h = act.do(A.activation, [m], L.eh[:, c, :], banks[c % 2], ACT.Relu, bias=e_b1[:, c:c + 1])
                done[c % 2] = [h]
            for t in range(TILES):
                for c in range(FF_CHUNKS):
                    m = pe.do(T.matmul, [h], banks[0][:, t * P:(t + 1) * P], lhsT=L.eh[:, c, t * P:(t + 1) * P],
                              rhs=e_w2[:, c, :], start=(c == 0), stop=(c == FF_CHUNKS - 1))
            bc = [P, TILES, DIM]
            m = dve.do(V.tensor_tensor, [m], out=L.r, in0=banks[0].rearrange("p (t n) -> p t n", t=TILES),
                       in1=e_b2[:].unsqueeze(1).to_broadcast(bc), op=ALU.add)
            m = dve.do(V.tensor_tensor, [m], out=L.r, in0=L.r, in1=L.xn, op=ALU.add)
            layer_norm(L, L.r, L.r, [m])
            m = dve.do(V.tensor_tensor, [L.normed], out=L.r, in0=L.r, in1=gamma[:].unsqueeze(1).to_broadcast(bc),
                       op=ALU.mult)
            m = dve.do(V.tensor_tensor, [m], out=L.r, in0=L.r, in1=beta[:].unsqueeze(1).to_broadcast(bc),
                       op=ALU.add)
            m = dve.do(V.scalar_tensor_tensor, [m], out=L.x[:], in0=L.r, scalar=0.5, in1=L.x[:],
                       op0=ALU.mult, op1=ALU.add)
            L.free = [m]

        def silu(src, th, dst, after):
            m = act.do(A.activation, after, th, src, ACT.Tanh, scale=0.5)
            m = dve.do(V.tensor_scalar, [m], out=th, in0=th, scalar1=0.5, scalar2=0.5, op0=ALU.mult, op1=ALU.add)
            m = dve.do(V.tensor_tensor, [m], out=dst, in0=src, in1=th, op=ALU.mult)
            return m

        def mamba(L):
            b0, b1 = L.banks[:, 0, :], L.banks[:, 1, :]
            both_banks = L.banks[:, :, :]
            layer_norm(L, L.x[:], L.xn, L.free)
            m = to_features(L, L.xn, b0, [L.normed])
            z = pool.do(G.memset, L.free, L.xc[:, :, 0:D_CONV - 1], 0.0)
            xT = act.do(A.activation, [m], L.hT[:], b0, ACT.Copy)
            for c, bank in enumerate((b0, b1)):
                m = pe.do(T.matmul, [xT], bank, lhsT=W_in[:, c * P:(c + 1) * P], rhs=L.hT[:], start=True, stop=True)
            xc = act.do(A.activation, [m, z], L.xc[:, :, D_CONV - 1:], both_banks, ACT.Copy)
            for c, bank in enumerate((b0, b1)):
                m = pe.do(T.matmul, [xc], bank, lhsT=W_in[:, D_INNER + c * P:D_INNER + (c + 1) * P], rhs=L.hT[:],
                          start=True, stop=True)
            gate = silu(both_banks, L.tmp, L.gate, [m])
            conv = [xc, xc]
            for j in range(D_CONV):
                nxt = []
                for c in range(CHUNKS):
                    tap = L.xc[:, c, j:j + SEQ]
                    if j == 0:
                        nxt.append(dve.do(V.tensor_scalar, conv[c:c + 1], out=L.dt[:, c, :], in0=tap,
                                          scalar1=conv_w[:, c, 0:1], scalar2=conv_b[:, c:c + 1],
                                          op0=ALU.mult, op1=ALU.add))
                    else:
                        nxt.append(dve.do(V.scalar_tensor_tensor, conv[c:c + 1], out=L.dt[:, c, :], in0=tap,
                                          scalar=conv_w[:, c, j:j + 1], in1=L.dt[:, c, :],
                                          op0=ALU.mult, op1=ALU.add))
                conv = nxt
            xs = silu(L.dt, L.tmp, L.xs, conv + [gate])
            for c in range(CHUNKS):
                m1 = pe.do(T.matmul, [xs], b0[0:DT_RANK, :], lhsT=W_x[:, c, 0:DT_RANK], rhs=L.xs[:, c, :],
                           start=(c == 0), stop=(c == CHUNKS - 1))
            for c in range(CHUNKS):
                m2 = pe.do(T.matmul, [], b1[0:32, :], lhsT=W_x[:, c, DT_RANK:DT_RANK + 32], rhs=L.xs[:, c, :],
                           start=(c == 0), stop=(c == CHUNKS - 1))
            dt_r = act.do(A.activation, [m1], L.hT[0:DT_RANK, :], b0[0:DT_RANK, :], ACT.Copy)
            bc = act.do(A.activation, [m2], L.bcs, b1[0:2 * D_STATE, :], ACT.Copy)
            rows_out = sp.dma(L.rows_out, [bc], L.rows_dram, L.bcs)
            for c, bank in enumerate((b0, b1)):
                m = pe.do(T.matmul, [dt_r, bc], bank, lhsT=W_dt[:, c * P:(c + 1) * P], rhs=L.hT[0:DT_RANK, :],
                          start=True, stop=True)
            dt_mm = m

            def fetch(n, after):
                i = n % 2
                sp.dma(L.rows_in[i], [rows_out] + after, L.Bs[i], L.rows_dram[n].partition_broadcast(P))
                return sp.dma(L.rows_in[i], [], L.Cs[i], L.rows_dram[D_STATE + n].partition_broadcast(P))

            fetched = [fetch(0, []), fetch(1, [dt_mm])]
            for c in range(CHUNKS):
                a = act.do(A.activation, [m, xs], L.tmp[:, c, :], L.banks[:, c, :], ACT.Abs, bias=b_dt[:, c:c + 1])
            a = act.do(A.activation, [a], L.tmp, L.tmp, ACT.Exp, scale=-1.0)
            a = act.do(A.activation, [a], L.tmp, L.tmp, ACT.Ln, bias=1.0)
            for c in range(CHUNKS):
                r = dve.do(V.tensor_scalar, [m, a], out=L.dt[:, c, :], in0=L.banks[:, c, :], scalar1=b_dt[:, c:c + 1],
                           scalar2=0.0, op0=ALU.add, op1=ALU.max)
            dt = dve.do(V.tensor_tensor, [r, a], out=L.dt, in0=L.dt, in1=L.tmp, op=ALU.add)
            z0 = dve.do(V.memset, [dt], L.dA[:, :, 0:1], 0.0)
            for c in range(CHUNKS):
                skipped = act.do(A.activation, conv + [xs], L.dBx[:, c, :], L.xs[:, c, :], ACT.Identity,
                                 scale=skipD[:, c:c + 1])
            dtx = dve.do(V.tensor_tensor, [dt, skipped], out=L.dtx, in0=L.dt, in1=L.xs, op=ALU.mult)
            sums = [b.rearrange("p (t c n) -> p t c n", t=2, c=CHUNKS) for b in (b0, b1)]
            both = [P, CHUNKS, SEQ]
            flat = lambda ap: ap.rearrange("p c n -> p (c n)")

            def gather(src, c, after, start, stop):
                for t in range(TILES):
                    m = pe.do(T.matmul, after if t == 0 else [], sums[t // 2][:, t % 2, c, :],
                              lhsT=src[:, c, t * P:(t + 1) * P], rhs=ident[:], is_transpose=True,
                              start=start and c == 0 and t % 2 == 0, stop=stop, skip_group_check=True)
                return m

            for c in range(CHUNKS):
                opened = gather(L.dBx, c, [skipped, dt], True, False)
            scanned, summed = [z0, opened], [rows_out]
            for n in range(D_STATE):
                i = n % 2
                for c in range(CHUNKS):
                    dA = act.do(A.activation, [dt] + scanned, L.dA[:, c, 1:], L.dt[:, c, 1:], ACT.Exp,
                                scale=negA[:, c, n:n + 1])
                m = dve.do(V.tensor_tensor, [fetched[i], dtx] + scanned, out=L.dBx,
                           in0=L.Bs[i].unsqueeze(1).to_broadcast(both), in1=L.dtx, op=ALU.mult)
                sc = dve.do(V.tensor_tensor_scan, [m, dA] + summed, out=flat(L.h), data0=flat(L.dA),
                            data1=flat(L.dBx), initial=0.0, op0=ALU.mult, op1=ALU.add)
                scanned = [sc]
                for c in range(CHUNKS):
                    hc = pool.do(G.tensor_tensor, [sc, fetched[i]], out=L.h[:, c, :], in0=L.h[:, c, :],
                                 in1=L.Cs[i], op=ALU.mult)
                    sm = gather(L.h, c, [hc], False, n == D_STATE - 1)
                summed = [sm]
                if n + 2 < D_STATE:
                    fetched[i] = fetch(n + 2, [hc, m])
            yT = L.h.rearrange("p c n -> p (c n)").rearrange("p (t c n) -> p t c n", t=TILES, c=CHUNKS)
            m = act.do(A.activation, [sm], yT.rearrange("p t c n -> p (t c n)"), both_banks, ACT.Copy)
            for c in range(CHUNKS):
                for t in range(TILES):
                    sm = pe.do(T.transpose, [m] if t == 0 else [], L.banks[:, c, t * P:(t + 1) * P],
                               yT[:, t, c, :], identity=ident[:])
            for c in range(CHUNKS):
                m = dve.do(V.tensor_tensor, [sm], out=L.gated[:, c, :], in0=L.banks[:, c, :], in1=L.gate[:, c, :],
                           op=ALU.mult)
            for t in range(TILES):
                for c in range(CHUNKS):
                    p = pe.do(T.matmul, [m], b0[:, t * P:(t + 1) * P], lhsT=L.gated[:, c, t * P:(t + 1) * P],
                              rhs=W_out[:, c, :], start=(c == 0), stop=(c == CHUNKS - 1))
            m = dve.do(V.tensor_tensor, [p], out=L.x[:], in0=b0.rearrange("p (t n) -> p t n", t=TILES),
                       in1=L.x[:], op=ALU.add)
            L.free = [m]

        def lane_program(i):
            L = lanes[i]
            stored = []
            for b in range(i, BATCH, LANES):
                if b >= LANES:
                    L.x_here = sp.dma(L.x_in, stored, L.x[:], x_dram[b])
                L.free = [L.x_here] + stored
                macaron_transformer(L)
                alibi_attention(L)
                macaron_transformer(L)
                expert_ffn(L)
                mamba(L)
                expert_ffn(L)
                stored = [sp.dma(L.x_out, L.free, out_dram[b], L.x[:])]
            L.stored = stored

        fill_queues(engines, [[e.taken() for e in engines]])
        programs = []
        for i in range(LANES):
            lane_program(i)
            programs.append([e.taken() for e in engines])
        fill_queues(engines, programs)
        sp.wait([m for L in lanes for m in L.stored])

        block = ctx.enter_context(nc.Block())

        @block.sync
        def _(eng):
            sp.play(eng)

        @block.tensor
        def _(eng):
            pe.play(eng)

        @block.vector
        def _(eng):
            dve.play(eng)

        @block.scalar
        def _(eng):
            act.play(eng)

        @block.gpsimd
        def _(eng):
            pool.play(eng)



_INS = ["L0_attn_x", "L0_attn_W_qk", "L0_attn_alibi_slope", "L0_ffn_wqkv", "L0_ffn_q_scale", "L0_ffn_k_scale",
        "L0_ffn_wo", "L0_ffn_w1", "L0_ffn_w2", "L0_ffn_b2",
        "L1_attn_W_in", "L1_attn_W_x", "L1_attn_W_dt", "L1_attn_W_out", "L1_ffn_w1", "L1_ffn_w2", "L1_ffn_b2",
        "L1_ffn_gamma", "L1_ffn_beta"]


def kernel(**inputs):
    import concourse.bacc as bacc
    from concourse.bass_utils import run_bass_kernel_spmd

    nc = bacc.Bacc("TRN2", target_bir_lowering=False, num_devices=1)
    arrays = {name: np.ascontiguousarray(inputs[name]) for name in _INS}
    arrays["WvT"] = np.ascontiguousarray(np.asarray(inputs["L0_attn_W_v"]).T)
    arrays["columns"] = parameter_columns(inputs)
    arrays.update(constant_tables())
    d = {n: nc.dram_tensor(f"in_{n}", a.shape, mybir.dt.from_np(a.dtype), kind="ExternalInput").ap()
         for n, a in arrays.items()}
    out = nc.dram_tensor("out_0", (BATCH, SEQ, DIM), F32, kind="ExternalOutput").ap()
    macaron_kernel(nc, d, out)
    r = run_bass_kernel_spmd(nc, [{f"in_{n}": a for n, a in arrays.items()}], core_ids=[0])
    return r.results[0]["out_0"]
```
